# Optimizing a Trainium2 kernel written in Bass

```python
import numpy as np
import jax
import jax.numpy as jnp

def _softmax(x, axis=-1):
    return jax.nn.softmax(x, axis=axis)

def _gelu(x):
    return jax.nn.gelu(x, approximate=True)

def _silu(x):
    return jax.nn.silu(x)

def _sigmoid(x):
    return jax.nn.sigmoid(x)

def _layernorm(x, axis=-1, eps=1e-05):
    m = jnp.mean(x, axis=axis, keepdims=True)
    v = jnp.var(x, axis=axis, keepdims=True)
    return (x - m) / jnp.sqrt(v + eps)

def _scatter_add(tgt, idx, src, axis=0):
    return tgt.at[idx].add(src)

def _segment_sum(src, seg, n):
    return jax.ops.segment_sum(src, seg, n)
kernel_name = 'mk_cond_seq_d1_seqx_r4_e2ad25'

def setup_inputs(seed: int=0):
    np.random.seed(seed)
    _w = jnp.asarray

    def _rec_inputs():
        import jax
        import jax.numpy as jnp
        _rk = jax.random.key(seed)
        x = -0.0005207 + 1.001 * jax.random.normal(jax.random.fold_in(_rk, 1), (2, 1024, 256), jnp.float32)
        _lenS = 1024 - jax.random.randint(jax.random.fold_in(_rk, 7), (2,), 0, max(1, 1024 // 4) + 1, jnp.int32)
        _lenS2 = 1024 - jax.random.randint(jax.random.fold_in(_rk, 8), (2,), 0, max(1, 1024 // 4) + 1, jnp.int32)
        itok_B_34_63 = jax.random.randint(jax.random.fold_in(_rk, 12), (2,), 34, 64, jnp.int32)
        fside_Bx16xSxS_0 = -1.47943e-05 + 1.00017 * jax.random.normal(jax.random.fold_in(_rk, 13), (2, 16, 1024, 1024), jnp.float32)
        _validS = jnp.arange(1024)[None, :] < _lenS[:, None]
        _validS2 = jnp.arange(1024)[None, :] < _lenS2[:, None]
        _causal = jnp.tril(jnp.ones((1024, 1024), dtype=bool))
        mask_Bx1xSxS_bk0 = jnp.logical_not(jnp.broadcast_to(_validS[:, None, None, :], (2, 1, 1024, 1024)))
        return (x, itok_B_34_63, fside_Bx16xSxS_0, mask_Bx1xSxS_bk0)
    x, itok_B_34_63, fside_Bx16xSxS_0, mask_Bx1xSxS_bk0 = _rec_inputs()

    def _L0_cond_setup():
        import jax, jax.numpy as jnp
        import numpy as np
        import math
        D_MODEL = 256
        N_HEAD = 16
        HEAD_DIM = D_MODEL // N_HEAD
        D_FF = 1024
        NUM_STEPS = 100.0
        RESCALE = 4000.0
        EPS = 1e-05

        def _sin_emb(t):
            half = D_MODEL // 2
            x = t.astype(jnp.float32) / NUM_STEPS * RESCALE
            freqs = jnp.exp(jnp.arange(half, dtype=jnp.float32) * (-math.log(10000.0) / (half - 1)))
            e = x[:, None] * freqs[None, :]
            return jnp.concatenate([jnp.sin(e), jnp.cos(e)], axis=-1)

        def _ln(x):
            m = jnp.mean(x, axis=-1, keepdims=True)
            v = jnp.var(x, axis=-1, keepdims=True)
            return (x - m) / jnp.sqrt(v + EPS)

        def _gelu2(x):
            return x * jax.nn.sigmoid(1.702 * x)
        key = jax.random.key(seed)
        ks = jax.random.split(key, 24)
        B, S, D, F = (4, 128, D_MODEL, D_FF)
        std = 0.02
        inp = {'src': jax.random.normal(ks[0], (B, S, D), dtype=jnp.float32), 'src_mask': jax.random.randint(ks[1], (B, 1, S, S), 0, 2).astype(bool), 'timestep': jax.random.randint(ks[2], (B,), 0, 100, dtype=jnp.int32), 'attention_bias': jax.random.normal(ks[3], (B, N_HEAD, S, S), dtype=jnp.float32), 'W_ada': jax.random.normal(ks[4], (D, 2 * D), dtype=jnp.float32) * std, 'b_ada': jnp.zeros((2 * D,), dtype=jnp.float32), 'Wq': jax.random.normal(ks[5], (D, D), dtype=jnp.float32) * std, 'bq': jnp.zeros((D,), dtype=jnp.float32), 'Wk': jax.random.normal(ks[6], (D, D), dtype=jnp.float32) * std, 'bk': jnp.zeros((D,), dtype=jnp.float32), 'Wv': jax.random.normal(ks[7], (D, D), dtype=jnp.float32) * std, 'bv': jnp.zeros((D,), dtype=jnp.float32), 'Wo': jax.random.normal(ks[8], (D, D), dtype=jnp.float32) * std, 'bo': jnp.zeros((D,), dtype=jnp.float32), 'W1': jax.random.normal(ks[9], (D, F), dtype=jnp.float32) * std, 'b1': jnp.zeros((F,), dtype=jnp.float32), 'W2': jax.random.normal(ks[10], (F, D), dtype=jnp.float32) * std, 'b2': jnp.zeros((D,), dtype=jnp.float32), 'g2': jnp.ones((D,), dtype=jnp.float32), 'beta2': jnp.zeros((D,), dtype=jnp.float32)}
        return inp
    _L0_cond_all = _L0_cond_setup()
    _L0_cond_in = {k: v for k, v in _L0_cond_all.items() if k in ('W_ada', 'b_ada', 'Wq', 'bq', 'Wk', 'bk', 'Wv', 'bv', 'Wo', 'bo', 'W1', 'b1', 'W2', 'b2', 'g2', 'beta2')}
    del _L0_cond_all
    return {'x': x, 'itok_B_34_63': itok_B_34_63, 'fside_Bx16xSxS_0': fside_Bx16xSxS_0, 'mask_Bx1xSxS_bk0': mask_Bx1xSxS_bk0, 'L0_cond_W_ada': _L0_cond_in['W_ada'], 'L0_cond_b_ada': _L0_cond_in['b_ada'], 'L0_cond_Wq': _L0_cond_in['Wq'], 'L0_cond_bq': _L0_cond_in['bq'], 'L0_cond_Wk': _L0_cond_in['Wk'], 'L0_cond_bk': _L0_cond_in['bk'], 'L0_cond_Wv': _L0_cond_in['Wv'], 'L0_cond_bv': _L0_cond_in['bv'], 'L0_cond_Wo': _L0_cond_in['Wo'], 'L0_cond_bo': _L0_cond_in['bo'], 'L0_cond_W1': _L0_cond_in['W1'], 'L0_cond_b1': _L0_cond_in['b1'], 'L0_cond_W2': _L0_cond_in['W2'], 'L0_cond_b2': _L0_cond_in['b2'], 'L0_cond_g2': _L0_cond_in['g2'], 'L0_cond_beta2': _L0_cond_in['beta2']}

def reference(x, itok_B_34_63, fside_Bx16xSxS_0, mask_Bx1xSxS_bk0, L0_cond_W_ada, L0_cond_b_ada, L0_cond_Wq, L0_cond_bq, L0_cond_Wk, L0_cond_bk, L0_cond_Wv, L0_cond_bv, L0_cond_Wo, L0_cond_bo, L0_cond_W1, L0_cond_b1, L0_cond_W2, L0_cond_b2, L0_cond_g2, L0_cond_beta2):
    import jax
    import jax.numpy as jnp

    def _L0_cond_ref(src, src_mask, timestep, attention_bias, W_ada, b_ada, Wq, bq, Wk, bk, Wv, bv, Wo, bo, W1, b1, W2, b2, g2, beta2):
        import jax, jax.numpy as jnp
        import numpy as np
        import math
        D_MODEL = 256
        N_HEAD = 16
        HEAD_DIM = D_MODEL // N_HEAD
        D_FF = 1024
        NUM_STEPS = 100.0
        RESCALE = 4000.0
        EPS = 1e-05

        def _sin_emb(t):
            half = D_MODEL // 2
            x = t.astype(jnp.float32) / NUM_STEPS * RESCALE
            freqs = jnp.exp(jnp.arange(half, dtype=jnp.float32) * (-math.log(10000.0) / (half - 1)))
            e = x[:, None] * freqs[None, :]
            return jnp.concatenate([jnp.sin(e), jnp.cos(e)], axis=-1)

        def _ln(x):
            m = jnp.mean(x, axis=-1, keepdims=True)
            v = jnp.var(x, axis=-1, keepdims=True)
            return (x - m) / jnp.sqrt(v + EPS)

        def _gelu2(x):
            return x * jax.nn.sigmoid(1.702 * x)
        B, S, D = src.shape
        emb = jax.nn.silu(_sin_emb(timestep)) @ W_ada + b_ada
        scale, shift = jnp.split(emb[:, None, :], 2, axis=-1)
        x = _ln(src) * (1.0 + scale) + shift
        q = (x @ Wq + bq).reshape(B, S, N_HEAD, HEAD_DIM).transpose(0, 2, 1, 3)
        k = (x @ Wk + bk).reshape(B, S, N_HEAD, HEAD_DIM).transpose(0, 2, 1, 3)
        v = (x @ Wv + bv).reshape(B, S, N_HEAD, HEAD_DIM).transpose(0, 2, 1, 3)
        scores = jnp.einsum('bhqd,bhkd->bhqk', q / math.sqrt(HEAD_DIM), k)
        scores = scores + attention_bias
        scores = jnp.where(src_mask, -jnp.inf, scores.astype(jnp.float32))
        probs = jax.nn.softmax(scores, axis=-1).astype(v.dtype)
        ctx = jnp.einsum('bhqk,bhkd->bhqd', probs, v)
        ctx = ctx.transpose(0, 2, 1, 3).reshape(B, S, D)
        x = x + (ctx @ Wo + bo)
        h = _ln(x) * g2 + beta2
        ff = _gelu2(h @ W1 + b1) @ W2 + b2
        return x + ff
    x = _L0_cond_ref(x, mask_Bx1xSxS_bk0, itok_B_34_63, fside_Bx16xSxS_0, L0_cond_W_ada, L0_cond_b_ada, L0_cond_Wq, L0_cond_bq, L0_cond_Wk, L0_cond_bk, L0_cond_Wv, L0_cond_bv, L0_cond_Wo, L0_cond_bo, L0_cond_W1, L0_cond_b1, L0_cond_W2, L0_cond_b2, L0_cond_g2, L0_cond_beta2)
    return x

_drawn_inputs = setup_inputs


def setup_inputs(seed=0):
    import zlib

    import numpy as np

    out = dict(_drawn_inputs(seed))
    spreads = {'L0_cond_b_ada': (0.0, 0.1),
     'L0_cond_bq': (0.0, 0.8),
     'L0_cond_bk': (0.0, 0.8),
     'L0_cond_bv': (0.0, 0.273),
     'L0_cond_bo': (0.0, 0.1),
     'L0_cond_b1': (0.0, 0.1),
     'L0_cond_b2': (0.0, 0.1),
     'L0_cond_g2': (1.0, 0.6),
     'L0_cond_beta2': (0.0, 0.79)}
    factors = {'fside_Bx16xSxS_0': 8.0, 'L0_cond_Wq': 8.0, 'L0_cond_Wk': 8.0, 'L0_cond_Wv': 3.413}
    for name, (base, spread) in spreads.items():
        noise = np.random.default_rng([zlib.crc32(name.encode()), seed]).standard_normal(out[name].shape)
        drawn = base * np.exp(spread * noise) if base else spread * noise
        out[name] = jnp.asarray(drawn.astype(out[name].dtype))
    for name, factor in factors.items():
        out[name] = (out[name] * factor).astype(out[name].dtype)
    return out
```

```python
import math
from contextlib import ExitStack

import numpy as np

import concourse.bass as bass
from concourse import mybir

P = 128
B, S, D, H, F = 2, 1024, 256, 16, 1024
HD = D // H
U = B * H
T = S // P
DC = D // P
FC = F // P
GT = 4
GN = GT * P
NG = S // GN
QK = 2 * DC
VW = 32
QUADS = 4
QW = S // QUADS
PARTS = 4
EPS = 1e-5
MASKED = -3.0e38
NO_KEY = 1.5e38
PE_MASK_TILE = 3
POOL_TILES = [t for t in range(T) if t != PE_MASK_TILE]
MAGIC = 1.5 * 2.0**23
TWO_PI_1 = 6.28125
TWO_PI_2 = round((2 * math.pi - TWO_PI_1) * 2**20) / 2**20
TWO_PI_3 = 2 * math.pi - TWO_PI_1 - TWO_PI_2
PI_BELOW = 3.1415925

F32 = mybir.dt.float32
F32R = mybir.dt.float32r
BF16 = mybir.dt.bfloat16
U8 = mybir.dt.uint8
I32 = mybir.dt.int32
ALU = mybir.AluOpType
ACT = mybir.ActivationFunctionType


def layer_kernel(nc, a, out):
    q_stacks = nc.dram_tensor("q_stacks", (U, PARTS * HD, S), F32, kind="Internal").ap()
    k_stacks = nc.dram_tensor("k_stacks", (U, PARTS * HD, S), F32, kind="Internal").ap()
    x1_dram = nc.dram_tensor("x1_dram", (B, S, D), F32, kind="Internal").ap()

    ctx = ExitStack()
    with ctx:
        def sb(name, shape, dt=F32):
            return ctx.enter_context(nc.sbuf_tensor(name, shape, dt))

        def sem(name):
            return ctx.enter_context(nc.semaphore(name))

        def wait_apart(engine, *waits):
            targets = [(semaphore, engine.to_reg(value)) for semaphore, value in waits]
            engine.wait_ge(consts_in, 16 * len(const_loads))
            for semaphore, register in targets:
                engine.wait_ge(semaphore, register)

        def as_row(name, n):
            return a[name].rearrange("(o n) -> o n", o=1).broadcast_to([P, n])

        def as_columns(name):
            return a[name].rearrange("(c p) -> p c", p=P)

        def as_chunks(name):
            return a[name].rearrange("(c p) n -> p c n", p=P)

        ident = sb("ident", [P, P])
        ident_bf = sb("ident_bf", [P, P], BF16)
        neg_mask = sb("neg_mask", [P, B, T, S], BF16)
        v_all = sb("v_all", [P, U, T, HD])
        ctx_all = sb("ctx_all", [P, B, T, D])
        ring = sb("ring", [P, T, S])
        q_st = sb("q_st", [P, 2, S], F32R)
        k_st = sb("k_st", [P, 2, S], F32R)
        v_st = sb("v_st", [P, 2, T, VW])
        big = sb("big", [P, 2, T, S])
        raw_ctx = sb("raw_ctx", [P, QW])
        neg_max = sb("neg_max", [P, 2, T])
        inv_sum = sb("inv_sum", [P, QW // P, QUADS])
        w_o = sb("w_o", [P, DC, D])
        w_1 = sb("w_1", [P, DC, F])
        w_2 = sb("w_2", [P, FC, D])
        b_o = sb("b_o", [P, D])
        b_2 = sb("b_2", [P, D])
        cols = sb("cols", [P, 2 * FC + 2 * DC])
        banks = ctx.enter_context(nc.psum_tensor("banks", [P, 8, 512], F32))

        big_words = big[:, :, :, :].rearrange("p a t s -> p (a t s)")
        taken = [0]

        def carve(*shape, dt=F32):
            n = int(np.prod(shape)) // (4 if dt == U8 else 1)
            flat = big_words[:, taken[0]:taken[0] + n]
            taken[0] += n
            assert taken[0] <= 2 * T * S
            if dt != F32:
                flat = flat.bitcast(dt)
            if len(shape) == 1:
                return flat
            names = "abc"[:len(shape)]
            sizes = dict(zip(names[1:], shape[1:]))
            return flat.rearrange(f"p ({' '.join(names)}) -> p {' '.join(names)}", **sizes)

        def over(row, n):
            return row.rearrange("p (o k) -> p o k", o=1).broadcast_to([P, n, row.shape[-1]])

        x_in = [carve(GT, D) for _ in range(NG)]
        xT = [carve(DC, GN) for _ in range(NG)]
        qk_f32 = [carve(GN) for _ in range(2)]
        qk_parts = [carve(2, GN, dt=F32R) for _ in range(2)]
        mask_u8 = carve(T, S, dt=U8)
        w_q, w_k, w_v = (carve(DC, D) for _ in range(3))
        w_ada = carve(DC, 2 * D)
        b_v = carve(D)
        b_ada = carve(2 * D)
        mod = carve(B, 2 * D)
        silu_wide = carve(DC * B, P)
        small = carve(128)
        freqs, b_q, b_k, b_qs = small[:, 0:1], small[:, 1:3], small[:, 3:5], small[:, 5:7]
        t_f, t_q, t_hi, t_lo = small[:, 8:10], small[:, 10:12], small[:, 12:14], small[:, 14:16]
        angle, turns, silu, e_neg = small[:, 16:20], small[:, 20:24], small[:, 24:28], small[:, 28:32]
        stats = small[:, 32:56].rearrange("p (c k) -> p c k", k=6)
        mean_var = [small[:, 56 + 8 * g:64 + 8 * g].rearrange("p (c k) -> p c k", k=2) for g in range(NG)]
        rstd = [small[:, 72 + 4 * g:76 + 4 * g] for g in range(NG)]
        t_i = sb("t_i", [P, B], I32)
        t_bf = sb("t_bf", [P, B], BF16)

        consts_in, w_in, ffn_w_in = sem("consts_in"), sem("w_in"), sem("ffn_w_in")
        x_in_ready = [sem(f"x_in_ready{g}") for g in range(NG)]
        x1_saved = [sem(f"x1_saved{g}") for g in range(NG)]
        mask_in, mask_done = sem("mask_in"), sem("mask_done")
        angle_ready, sin_ready, en_ready = sem("angle_ready"), sem("sin_ready"), sem("en_ready")
        silu_ready, ada_ready = sem("silu_ready"), sem("ada_ready")
        var_ready, std_ready, x1_ready = sem("var_ready"), sem("std_ready"), sem("x1_ready")
        xT_ready, xT_saved = sem("xT_ready"), sem("xT_saved")
        qk_ready, qk_copied, qk_split = sem("qk_ready"), sem("qk_copied"), sem("qk_split")
        parts_saved = [sem(f"parts_saved{i}") for i in range(2)]
        v_ready, v_saved = sem("v_ready"), sem("v_saved")
        dve_step, pool_step = sem("dve_step"), sem("pool_step")
        bias_in = [sem(f"bias_in{t}") for t in range(T)]

        def load_bias(sp, u, t):
            sp.dma_start(ring[:, t, :], a["bias"][u, t * P:(t + 1) * P, :]).then_inc(bias_in[t], 16)

        const_loads = [
            (t_i[:, :], as_row("itok", B)), (freqs, a["freqs"].rearrange("(p o) -> p o", o=1)),
            (ident[:, :], a["ident"]), (b_ada, as_row("b_ada", 2 * D)), (b_v, as_row("bv", D)),
            (b_q, as_columns("bq")), (b_k, as_columns("bk")), (w_ada, as_chunks("W_ada")),
        ]
        b_1, b_1s = cols[:, 0:FC], cols[:, FC:2 * FC]
        g_2, beta_2 = cols[:, 2 * FC:2 * FC + DC], cols[:, 2 * FC + DC:]
        ffn_loads = [
            (w_o[:, :, :], as_chunks("Wo")), (w_1[:, :, :], as_chunks("W1")), (w_2[:, :, :], as_chunks("W2")),
            (b_o[:, :], as_row("bo", D)), (b_2[:, :], as_row("b2", D)), (b_1, as_columns("b1")),
            (g_2, as_columns("g2")), (beta_2, as_columns("beta2")),
        ]

        with nc.Block() as block:

            @block.sync
            def _(sp):
                for dst, src in const_loads:
                    sp.dma_start(dst, src, allow_slow_non_contiguous=True).then_inc(consts_in, 16)
                with sp.Fori(0, B) as b:
                    sp.wait_ge(xT_ready, NG * b + NG)
                    for g in range(NG):
                        sp.wait_ge(x1_saved[g], 16 * b + 16)
                        sp.dma_start(x_in[g],
                                     a["x"][b, g * GN:(g + 1) * GN, :].rearrange("(c p) d -> p c d", p=P))\
                          .then_inc(x_in_ready[g], 16)
                    wait_apart(sp, (mask_done, b + 1))
                    sp.dma_start(mask_u8, a["mask"][b, :, :].rearrange("(t p) k -> p t k", p=P))\
                      .then_inc(mask_in, 16)
                    for g in range(NG):
                        sp.wait_ge(x1_ready, NG * b + g + 1)
                        sp.dma_start(x1_dram[b, g * GN:(g + 1) * GN, :].rearrange("(c p) d -> p c d", p=P),
                                     x_in[g]).then_inc(x1_saved[g], 16)
                        for n in range(QK):
                            sp.wait_ge(qk_split, 2 + QK * NG * b + QK * g + n + 1)
                            dst = (q_stacks, k_stacks)[n // DC]
                            first_head = b * H + (n % DC) * (H // DC)
                            for r in range(PARTS):
                                part = (r // 2, r % 2)[n // DC]
                                sp.dma_start(dst[bass.ds(first_head, H // DC), r * HD:(r + 1) * HD,
                                                 g * GN:(g + 1) * GN],
                                             qk_parts[n % 2][:, part, :].bitcast(F32))\
                                  .then_inc(parts_saved[n % 2], 16)
                for t in range(T):
                    load_bias(sp, 0, t)
                for g in range(NG):
                    sp.wait_ge(x1_saved[g], 16 * (B + 1))
                for i in range(2):
                    sp.wait_ge(parts_saved[i], 16 * PARTS * (1 + B * NG * QK // 2))

            @block.gpsimd
            def _(pool):
                for w, name in ((w_q, "Wq"), (w_k, "Wk"), (w_v, "Wv")):
                    pool.dma_start(w, as_chunks(name)).then_inc(w_in, 16)
                pool.memset(q_st[:, :, :].bitcast(F32), 0.0)
                pool.memset(k_st[:, :, :].bitcast(F32), 0.0)
                pool.memset(v_st[:, :, :, :], 0.0).then_inc(pool_step, 1)
                pool.wait_ge(pool_step, 1)
                pool.memset(v_st[:, :, :, HD:HD + 1], 1.0)
                pool.wait_ge(consts_in, 16 * len(const_loads))
                pool.tensor_copy(ident_bf[:, :], ident[:, :])
                for dst, src in ffn_loads:
                    pool.dma_start(dst, src, allow_slow_non_contiguous=True).then_inc(ffn_w_in, 16)

            @block.scalar
            def _(act):
                act.sem_inc(mask_done, 1)
                for g in range(NG):
                    act.sem_inc(x1_saved[g], 16)
                act.wait_ge(angle_ready, 1)
                act.activation(silu, angle, ACT.Sin).then_inc(sin_ready, 1)
                act.wait_ge(sin_ready, 1)
                act.activation(e_neg, silu, ACT.Exp, scale=-1.0).then_inc(en_ready, 1)
                with act.Fori(0, B) as b:
                    for g in range(NG):
                        act.wait_ge(var_ready, NG * b + g + 1)
                        act.activation(rstd[g], mean_var[g][:, :, 1], ACT.Sqrt).then_inc(std_ready, 1)
                    act.wait_ge(mask_in, 16 * b + 16)
                    act.activation(neg_mask[:, bass.ds(b, 1), :, :].rearrange("p o t k -> p (o t) k"), mask_u8,
                                   ACT.Copy, scale=MASKED).then_inc(mask_done, 1)
                    for g in range(NG):
                        act.wait_ge(xT_ready, NG + NG * b + g + 1)
                        for c in range(DC):
                            act.activation(xT[g][:, c, :], banks[:, c, :], ACT.Copy).then_inc(xT_saved, 1)
                        for n in range(QK):
                            k = QK * NG * b + QK * g + n
                            act.wait_ge(qk_ready, k + 1)
                            act.wait_ge(qk_split, k + 1)
                            act.activation(qk_f32[n % 2], banks[:, 2 + n % 2, :], ACT.Identity,
                                           bias=(b_qs, b_k)[n // DC][:, n % DC:n % DC + 1],
                                           scale=(HD ** -0.5, 1.0)[n // DC]).then_inc(qk_copied, 1)

            @block.vector
            def _(dve):
                steps = [0, 0]

                def step(instruction):
                    instruction.then_inc(dve_step, 1)
                    steps[1] += 1
                    dve.wait_ge(dve_step, steps[0] + steps[1])

                def step_apart(instruction):
                    instruction.then_inc(dve_step, 1)
                    steps[1] += 1
                    wait_apart(dve, (dve_step, steps[0] + steps[1]))

                dve.sem_inc(qk_split, 2)
                dve.sem_inc(v_saved, 2)
                for i in range(2):
                    dve.sem_inc(parts_saved[i], 16 * PARTS)
                dve.wait_ge(consts_in, 16 * len(const_loads))
                step(nc.vector.tensor_copy(t_f, t_i[:, :]))
                step(nc.vector.tensor_scalar(t_q, t_f, 0.01, None, ALU.mult))
                step(nc.vector.tensor_copy(t_bf[:, :], t_q))
                step(nc.vector.tensor_tensor(t_lo, t_q, t_bf[:, :], ALU.subtract))
                step(nc.vector.scalar_tensor_tensor(t_hi, t_bf[:, :], -100.0, t_f, ALU.mult, ALU.add))
                step(nc.vector.scalar_tensor_tensor(t_hi, t_lo, -100.0, t_hi, ALU.mult, ALU.add))
                step(nc.vector.scalar_tensor_tensor(t_q, t_hi, 0.01, t_q, ALU.mult, ALU.add))
                for c in range(DC):
                    step(nc.vector.tensor_scalar(angle[:, c * B:(c + 1) * B], t_q, 4000.0, freqs,
                                                 ALU.mult, ALU.mult))
                step(nc.vector.tensor_scalar(turns, angle, 1 / (2 * math.pi), None, ALU.mult))
                step(nc.vector.tensor_scalar(turns[:, B:], turns[:, B:], 0.25, None, ALU.add))
                step(nc.vector.tensor_scalar(turns, turns, MAGIC, None, ALU.add))
                step(nc.vector.tensor_scalar(turns, turns, -MAGIC, None, ALU.add))
                for part in (TWO_PI_1, TWO_PI_2, TWO_PI_3):
                    step(nc.vector.scalar_tensor_tensor(angle, turns, -part, angle, ALU.mult, ALU.add))
                step(nc.vector.tensor_scalar(angle[:, B:], angle[:, B:], math.pi / 2, None, ALU.add))
                nc.vector.tensor_scalar(angle, angle, PI_BELOW, -PI_BELOW, ALU.min, ALU.max)\
                  .then_inc(angle_ready, 1)
                dve.wait_ge(en_ready, 1)
                step(nc.vector.tensor_scalar(e_neg, e_neg, 1.0, None, ALU.add))
                step(nc.vector.reciprocal(e_neg, e_neg))
                step(nc.vector.tensor_tensor(silu, silu, e_neg, ALU.mult))
                nc.vector.tensor_copy(silu_wide, silu.rearrange("p (c o) -> p c o", o=1)
                                      .broadcast_to([P, DC * B, P])).then_inc(silu_ready, 1)
                step(nc.vector.tensor_scalar(b_qs, b_q, HD ** -0.5, None, ALU.mult))
                for i in range(B):
                    dve.wait_ge(ada_ready, i + 1)
                    step(nc.vector.tensor_tensor(mod[:, i, :], banks[:, 6 + i, :], b_ada, ALU.add))
                step(nc.vector.tensor_scalar(mod[:, :, 0:D], mod[:, :, 0:D], 1.0, None, ALU.add))
                before, per_batch = steps[1], NG * (2 + 3) + NG * QK
                with dve.Fori(0, B) as b:
                    steps[0], steps[1] = before + b * per_batch, 0
                    scale_row = mod[:, bass.ds(b, 1), 0:D].broadcast_to([P, GT, D])
                    shift_row = mod[:, bass.ds(b, 1), D:2 * D].broadcast_to([P, GT, D])
                    for g in range(NG):
                        dve.wait_ge(x_in_ready[g], 16 * b + 16)
                        for c in range(GT):
                            last = nc.vector.bn_stats(stats[:, c, :], x_in[g][:, c, :])
                        step_apart(last)
                        for c in range(GT):
                            last = nc.vector.bn_aggr(mean_var[g][:, c, :], stats[:, c, :])
                        step(last)
                        nc.vector.tensor_scalar(mean_var[g][:, :, 1], mean_var[g][:, :, 1], EPS, None, ALU.add)\
                          .then_inc(var_ready, 1)
                    for g in range(NG):
                        dve.wait_ge(std_ready, NG * b + g + 1)
                        step(nc.vector.reciprocal(rstd[g], rstd[g]))
                        for c in range(GT):
                            last = nc.vector.tensor_scalar(x_in[g][:, c, :], x_in[g][:, c, :],
                                                           mean_var[g][:, c, 0:1], rstd[g][:, c:c + 1],
                                                           ALU.subtract, ALU.mult)
                        step(last)
                        step(nc.vector.tensor_tensor(x_in[g], x_in[g], scale_row, ALU.mult))
                        nc.vector.tensor_tensor(x_in[g], x_in[g], shift_row, ALU.add).then_inc(x1_ready, 1)
                    for g in range(NG):
                        for n in range(QK):
                            k = QK * NG * b + QK * g + n
                            dve.wait_ge(qk_copied, 2 + k + 1)
                            dve.wait_ge(parts_saved[n % 2],
                                        16 * PARTS * (QK * NG // 2 * b + QK // 2 * g + n // 2 + 1))
                            hi, lo = (qk_parts[n % 2][:, i, :] for i in range(2))
                            step(nc.vector.tensor_copy(hi, qk_f32[n % 2]))
                            nc.vector.tensor_tensor(lo, qk_f32[n % 2], hi.bitcast(F32), ALU.subtract)\
                              .then_inc(qk_split, 1)
                        for i in range(2):
                            dve.wait_ge(v_ready, 2 * NG * b + 2 * g + i + 1)
                            kt = g * GT + 2 * i
                            nc.vector.tensor_tensor(
                                v_all[:, bass.ds(b * H, H), kt:kt + 2, :].rearrange("p h t d -> p t h d"),
                                banks[:, 4 + i, :].rearrange("p (t h d) -> p t h d", t=2, h=H),
                                over(b_v, 2).rearrange("p t (h d) -> p t h d", h=H),
                                ALU.add).then_inc(v_saved, 1)
                    assert steps[1] == per_batch

            @block.tensor
            def _(pe):
                pe.sem_inc(xT_ready, NG)
                pe.sem_inc(xT_saved, DC)
                pe.sem_inc(qk_copied, 2)
                pe.wait_ge(silu_ready, 1)
                pe.wait_ge(consts_in, 16 * len(const_loads))
                for i in range(B):
                    for c in range(DC):
                        last = nc.tensor.matmul(banks[:, 6 + i, :], silu_wide[:, c * B + i, :], w_ada[:, c, :],
                                                start=(c == 0), stop=(c == DC - 1))
                    last.then_inc(ada_ready, 1)
                pe.wait_ge(w_in, 16 * 3)
                with pe.Fori(0, B) as b:
                    for g in range(NG):
                        pe.wait_ge(x1_ready, NG * b + g + 1)
                        pe.wait_ge(xT_saved, DC * NG * b + DC * g + DC)
                        for c in range(DC):
                            for i in range(GT):
                                last = nc.tensor.transpose(banks[:, c, i * P:(i + 1) * P],
                                                           x_in[g][:, i, c * P:(c + 1) * P], ident[:, :])
                        last.then_inc(xT_ready, 1)
                        pe.wait_ge(xT_saved, DC * NG * b + DC * g + 2 * DC)
                        for n in range(QK):
                            w, c = (w_q, w_k)[n // DC], n % DC
                            pe.wait_ge(qk_copied, QK * NG * b + QK * g + n + 1)
                            for kc in range(DC):
                                last = nc.tensor.matmul(banks[:, 2 + n % 2, :], w[:, kc, c * P:(c + 1) * P],
                                                        xT[g][:, kc, :], start=(kc == 0), stop=(kc == DC - 1))
                            last.then_inc(qk_ready, 1)
                        for i in range(2):
                            pe.wait_ge(v_saved, 2 * NG * b + 2 * g + i + 1)
                            for j in range(2):
                                t = 2 * i + j
                                for kc in range(DC):
                                    last = nc.tensor.matmul(banks[:, 4 + i, j * D:(j + 1) * D],
                                                            xT[g][:, kc, t * P:(t + 1) * P], w_v[:, kc, :],
                                                            start=(kc == 0), stop=(kc == DC - 1))
                            last.then_inc(v_ready, 1)

        stacks_in = [sem(f"stacks_in{i}") for i in range(2)]
        masked = sem("masked")
        scores_ready = sem("scores_ready")
        shifted = sem("shifted")
        probs_ready = sem("probs_ready")
        pt_ready = [sem(f"pt_ready{i}") for i in range(2)]
        pt_saved = [sem(f"pt_saved{i}") for i in range(2)]
        v_staged = sem("v_staged")
        pv_done = sem("pv_done")
        raw_saved = sem("raw_saved")
        back_ready = sem("back_ready")
        inv_ready, ctx_stored = sem("inv_ready"), sem("ctx_stored")
        pts = [big[:, i, :, :] for i in range(2)]
        LEAD = 2
        HALF = T // 2

        def head_pairs(engine, first, end, emit):
            assert first % 2 == 0 and end % 2 == 0
            with engine.Fori(0, (end - first) // 2) as i:
                for parity in range(2):
                    emit(2 * i + first + parity, parity)

        with nc.Block() as block:

            @block.sync
            def _(sp):
                def load_stacks(u, parity):
                    for src, dst in ((q_stacks, q_st), (k_stacks, k_st)):
                        sp.dma_start(dst[0:PARTS * HD, parity, :].bitcast(F32), src[u, :, :])\
                          .then_inc(stacks_in[parity], 16)

                def head(u, parity):
                    sp.wait_ge(scores_ready, T * u - T)
                    load_stacks(u, parity)
                    for t in range(T):
                        sp.wait_ge(pt_ready[1], T + T * u - T + t + 1)
                        load_bias(sp, u, t)

                load_stacks(0, 0)
                load_stacks(1, 1)
                for t in range(T):
                    sp.wait_ge(pt_ready[1], T + t + 1)
                    load_bias(sp, 1, t)
                head_pairs(sp, 2, U, head)

            @block.gpsimd
            def _(pool):
                def head(u, parity):
                    for t in POOL_TILES:
                        pool.wait_ge(bias_in[t], 16 * u + 16)
                        pool.tensor_tensor(
                            ring[:, t, :], ring[:, t, :],
                            neg_mask[:, bass.ds(u // H, 1), t, :].rearrange("p o k -> p (o k)"),
                            ALU.add).then_inc(masked, 1)

                head_pairs(pool, 0, U, head)

            @block.vector
            def _(dve):
                def normalise(u):
                    back = banks[:, 7, 0:QW].rearrange("p (i j w) -> p i j w", i=QW // P, j=QUADS)
                    dve.wait_ge(back_ready, u + 2)
                    nc.vector.reciprocal(inv_sum[:, :, :], back[:, :, :, HD]).then_inc(inv_ready, 1)
                    dve.wait_ge(inv_ready, u + 1)
                    dst = ctx_all[:, bass.ds(u // H, 1), :, bass.ds((u % H) * HD, HD)]\
                        .rearrange("p o (j i) d -> p (o i) j d", i=QW // P)
                    nc.vector.tensor_tensor(
                        dst, back[:, :, :, 0:HD],
                        inv_sum[:, :, :].rearrange("p i (j o) -> p i j o", o=1)
                        .broadcast_to([P, QW // P, QUADS, HD]),
                        ALU.mult).then_inc(ctx_stored, 1)

                def shift(u, parity, t):
                    s = 2 * (t % 2)
                    if t == PE_MASK_TILE:
                        bias = bias_in[t], 16 * u + 16
                    else:
                        bias = masked, len(POOL_TILES) * u + POOL_TILES.index(t) + 1
                    wait_apart(dve, bias, (scores_ready, T * u + t + 1))
                    nc.vector.tensor_tensor_reduce(
                        out=ring[:, t, :], in0=banks[:, s:s + 2, :].rearrange("p b n -> p (b n)"),
                        in1=ring[:, t, :], scale=-1.0, scalar=NO_KEY, op0=ALU.add, op1=ALU.min,
                        accum_out=neg_max[:, parity, t:t + 1]).then_inc(shifted, 1)

                def head(u, parity, normalises=True, ahead=True):
                    for t in range(T):
                        if t == 0:
                            dve.wait_ge(pv_done, u + 1)
                        if t == 2 and normalises:
                            normalise(u - 2)
                        if t + LEAD < T:
                            shift(u, parity, t + LEAD)
                        elif ahead:
                            shift(u + 1, 1 - parity, t + LEAD - T)
                        dve.wait_ge(pt_ready[1], T + T * u + t + 1)
                        nc.vector.tensor_copy(pts[parity][:, HALF:T, t * P:(t + 1) * P],
                                              banks[:, 5, :].rearrange("p (k q) -> p k q", k=HALF))\
                          .then_inc(pt_saved[1], 1)

                dve.sem_inc(ctx_stored, 1)
                dve.sem_inc(shifted, LEAD)
                for t in range(LEAD):
                    shift(0, 0, t)
                head(0, 0, normalises=False)
                head(1, 1, normalises=False)
                head_pairs(dve, 2, U - 2, head)
                head(U - 2, 0)
                head(U - 1, 1, ahead=False)
                normalise(U - 2)
                normalise(U - 1)

            @block.scalar
            def _(act):
                def save_raw(u):
                    act.wait_ge(pv_done, u + 3)
                    act.wait_ge(back_ready, u + 1)
                    act.activation(raw_ctx[:, :], banks[:, 6, 0:QW], ACT.Copy).then_inc(raw_saved, 1)

                def exponentials(u, parity, t):
                    act.wait_ge(shifted, LEAD + T * u + t + 1)
                    act.activation(ring[:, t, :], ring[:, t, :], ACT.Exp, scale=-1.0,
                                   bias=neg_max[:, parity, t:t + 1]).then_inc(probs_ready, 1)

                def head(u, parity, saves=True, ahead=True):
                    for t in range(T):
                        if t + 1 < T:
                            exponentials(u, parity, t + 1)
                        elif ahead:
                            exponentials(u + 1, 1 - parity, 0)
                        if t == 0:
                            act.wait_ge(pv_done, u + 1)
                            if saves:
                                save_raw(u - 2)
                            act.activation(
                                v_st[:, parity, :, 0:HD],
                                v_all[:, bass.ds(u, 1), :, :].rearrange("p o t d -> p (o t) d"),
                                ACT.Copy).then_inc(v_staged, 1)
                        act.wait_ge(pt_ready[0], T * u + t + 1)
                        act.activation(pts[parity][:, 0:HALF, t * P:(t + 1) * P],
                                       banks[:, 4, :].rearrange("p (k q) -> p k q", k=HALF),
                                       ACT.Copy).then_inc(pt_saved[0], 1)

                act.sem_inc(raw_saved, 1)
                for i in range(2):
                    act.sem_inc(pt_saved[i], 1)
                exponentials(0, 0, 0)
                head(0, 0, saves=False)
                head(1, 1, saves=False)
                head_pairs(act, 2, U - 2, head)
                head(U - 2, 0)
                head(U - 1, 1, ahead=False)
                save_raw(U - 2)
                save_raw(U - 1)

            @block.tensor
            def _(pe):
                def scores(u, parity, t):
                    s = 2 * (t % 2)
                    if t == 0:
                        pe.wait_ge(stacks_in[parity], 32 * (u // 2) + 32)
                    pe.wait_ge(shifted, T * u + t + 1)
                    for c in range(S // 512):
                        by_pe = t == PE_MASK_TILE
                        last = nc.tensor.matmul(banks[:, s + c, :], q_st[:, parity, t * P:(t + 1) * P],
                                                k_st[:, parity, c * 512:(c + 1) * 512],
                                                start=True, stop=not by_pe)
                        if by_pe:
                            mask = neg_mask[:, bass.ds(u // H, 1), t, c * 512:(c + 1) * 512]
                            last = nc.tensor.matmul(banks[:, s + c, :], ident_bf[:, :],
                                                    mask.rearrange("p o k -> p (o k)"), start=False, stop=True)
                    last.then_inc(scores_ready, 1)

                def transposes(u, t):
                    pe.wait_ge(probs_ready, T * u + t + 1)
                    for half in range(2):
                        pe.wait_ge(pt_saved[half], T * u + t + 1)
                        for k in range(HALF):
                            kt = half * HALF + k
                            last = nc.tensor.transpose(banks[:, 4 + half, k * P:(k + 1) * P],
                                                       ring[:, t, kt * P:(kt + 1) * P], ident[:, :])
                        last.then_inc(pt_ready[half], 1)

                def values(u, parity, kt):
                    if kt == 0:
                        for half in range(2):
                            pe.wait_ge(pt_saved[half], T * u + T + 1)
                        pe.wait_ge(v_staged, u + 1)
                        pe.wait_ge(raw_saved, u + 1)
                    for j in range(QUADS):
                        last = nc.tensor.matmul(banks[VW * j:VW * (j + 1), 6, 0:QW], v_st[:, parity, kt, :],
                                                pts[parity][:, kt, j * QW:(j + 1) * QW],
                                                start=(kt == 0), stop=(kt == T - 1))
                    if kt == T - 1:
                        last.then_inc(pv_done, 1)

                def back(u):
                    pe.wait_ge(raw_saved, u + 2)
                    pe.wait_ge(ctx_stored, u + 1)
                    for i in range(QW // P):
                        last = nc.tensor.transpose(banks[:, 7, i * P:(i + 1) * P],
                                                   raw_ctx[:, i * P:(i + 1) * P], ident[:, :])
                    last.then_inc(back_ready, 1)

                def head(u, parity, ahead=True, before=1):
                    for t in range(T):
                        if t + LEAD < T:
                            scores(u, parity, t + LEAD)
                        elif ahead:
                            scores(u + 1, 1 - parity, t + LEAD - T)
                        transposes(u, t)
                        if t == 1 and before >= 2:
                            back(u - 2)
                        if before >= 1:
                            values(u - 1, 1 - parity, t)

                pe.sem_inc(pt_ready[1], T)
                pe.sem_inc(pv_done, 2)
                pe.sem_inc(back_ready, 1)
                for t in range(LEAD):
                    scores(0, 0, t)
                head(0, 0, before=0)
                head(1, 1, before=1)
                head_pairs(pe, 2, U - 2, lambda u, parity: head(u, parity, before=2))
                head(U - 2, 0, before=2)
                head(U - 1, 1, ahead=False, before=2)
                back(U - 2)
                for kt in range(T):
                    values(U - 1, 1, kt)
                back(U - 1)

        taken[0] = 0
        ctx_in = ring[:, 0:2, :].rearrange("p a (t d) -> p (a t) d", d=D)
        x2 = [carve(GT, D) for _ in range(NG)]
        xn = [carve(GT, D) for _ in range(NG)]
        ctxT = [carve(DC, GN) for _ in range(NG)]
        hT = [carve(DC, GN) for _ in range(NG)]
        gated = [carve(FC, GN) for _ in range(NG)]
        work = sb("work", [P, 64])
        sig = [ring[:, 2 + i, 0:GN] for i in range(2)]
        stats3 = work[:, 0:24].rearrange("p (c k) -> p c k", k=6)
        mean_var3 = [work[:, 24 + 8 * g:32 + 8 * g].rearrange("p (c k) -> p c k", k=2) for g in range(NG)]
        rstd3 = [work[:, 40 + 4 * g:44 + 4 * g] for g in range(NG)]

        ctx_in_ready, x1_back = sem("ctx_in_ready"), [sem(f"x1_back{g}") for g in range(NG)]
        ctxT_ready, ctxT_saved = sem("ctxT_ready"), sem("ctxT_saved")
        x1_biased, proj_ready, x2_ready = sem("x1_biased"), sem("proj_ready"), sem("x2_ready")
        var3_ready, std3_ready, xn_ready = sem("var3_ready"), sem("std3_ready"), sem("xn_ready")
        hT_ready, hT_saved = sem("hT_ready"), sem("hT_saved")
        up_ready, sig_ready, gated_ready = sem("up_ready"), sem("sig_ready"), sem("gated_ready")
        down_ready, x2_biased, y_ready = sem("down_ready"), sem("x2_biased"), sem("y_ready")
        stored = [sem(f"stored{g}") for g in range(NG)]
        dve_step3, b_1s_ready = sem("dve_step3"), sem("b_1s_ready")

        def token_rows(dram, b, g):
            return dram[b, g * GN:(g + 1) * GN, :].rearrange("(c p) d -> p c d", p=P)

        with nc.Block() as block:

            @block.sync
            def _(sp):
                with sp.Fori(0, B) as b:
                    sp.wait_ge(ctxT_ready, NG * b + NG)
                    sp.dma_start(ctx_in, ctx_all[:, bass.ds(b, 1), :, :].rearrange("p o t d -> p (o t) d")).then_inc(ctx_in_ready, 16)
                    for g in range(NG):
                        sp.wait_ge(stored[g], 16 * b + 16)
                        sp.dma_start(x2[g], token_rows(x1_dram, b, g)).then_inc(x1_back[g], 16)
                    for g in range(NG):
                        sp.wait_ge(y_ready, 2 + 2 * NG * b + 2 * g + 2)
                        sp.dma_start(token_rows(out, b, g), x2[g]).then_inc(stored[g], 16)
                for g in range(NG):
                    sp.wait_ge(stored[g], 16 * (B + 1))

            @block.gpsimd
            def _(pool):
                pool.wait_ge(ffn_w_in, 16 * len(ffn_loads))
                with pool.Fori(0, B) as b:
                    for g in range(NG):
                        pool.wait_ge(x1_back[g], 16 * b + 16)
                        pool.tensor_tensor(x2[g], x2[g], over(b_o[:, :], GT), ALU.add).then_inc(x1_biased, 1)
                    for g in range(NG):
                        pool.wait_ge(xn_ready, NG * b + g + 1)
                        pool.tensor_tensor(x2[g], x2[g], over(b_2[:, :], GT), ALU.add).then_inc(x2_biased, 1)

            @block.scalar
            def _(act):
                act.wait_ge(b_1s_ready, 1)
                act.sem_inc(sig_ready, 2)
                with act.Fori(0, B) as b:
                    for g in range(NG):
                        act.wait_ge(ctxT_ready, NG + NG * b + g + 1)
                        for c in range(DC):
                            act.activation(ctxT[g][:, c, :], banks[:, c, :], ACT.Copy).then_inc(ctxT_saved, 1)
                    for g in range(NG):
                        act.wait_ge(var3_ready, NG * b + g + 1)
                        act.activation(rstd3[g], mean_var3[g][:, :, 1], ACT.Sqrt).then_inc(std3_ready, 1)
                    for g in range(NG):
                        act.wait_ge(hT_ready, NG * b + g + 1)
                        for c in range(DC):
                            act.activation(hT[g][:, c, :], banks[:, c, :], ACT.Identity,
                                           scale=g_2[:, c:c + 1], bias=beta_2[:, c:c + 1]).then_inc(hT_saved, 1)
                        for f in range(FC):
                            n = FC * NG * b + FC * g + f
                            act.wait_ge(up_ready, n + 1)
                            act.wait_ge(gated_ready, n + 1)
                            act.activation(sig[f % 2], banks[:, 4 + f % 2, :], ACT.Sigmoid, scale=1.702,
                                           bias=b_1s[:, f:f + 1]).then_inc(sig_ready, 1)

            @block.vector
            def _(dve):
                steps = [0, 0]

                def step(instruction):
                    instruction.then_inc(dve_step3, 1)
                    steps[1] += 1
                    dve.wait_ge(dve_step3, steps[0] + steps[1])

                def step_apart(instruction):
                    instruction.then_inc(dve_step3, 1)
                    steps[1] += 1
                    wait_apart(dve, (dve_step3, steps[0] + steps[1]))

                for g in range(NG):
                    dve.sem_inc(stored[g], 16)
                dve.sem_inc(gated_ready, 2)
                dve.sem_inc(x2_ready, 2)
                dve.sem_inc(y_ready, 2)
                dve.wait_ge(ffn_w_in, 16 * len(ffn_loads))
                nc.vector.tensor_scalar(b_1s, b_1, 1.702, None, ALU.mult).then_inc(b_1s_ready, 1)
                per_batch = NG * 3
                with dve.Fori(0, B) as b:
                    steps[0], steps[1] = b * per_batch, 0
                    for g in range(NG):
                        dve.wait_ge(x1_biased, NG * b + g + 1)
                        for i in range(2):
                            dve.wait_ge(proj_ready, 2 * NG * b + 2 * g + i + 1)
                            last = nc.vector.tensor_tensor(
                                x2[g][:, 2 * i:2 * i + 2, :],
                                banks[:, 2 + i, :].rearrange("p (c d) -> p c d", c=2),
                                x2[g][:, 2 * i:2 * i + 2, :], ALU.add)
                            last.then_inc(x2_ready, 1)
                        dve.wait_ge(x2_ready, 2 + 2 * NG * b + 2 * g + 2)
                        for c in range(GT):
                            last = nc.vector.bn_stats(stats3[:, c, :], x2[g][:, c, :])
                        step_apart(last)
                        for c in range(GT):
                            last = nc.vector.bn_aggr(mean_var3[g][:, c, :], stats3[:, c, :])
                        step(last)
                        nc.vector.tensor_scalar(mean_var3[g][:, :, 1], mean_var3[g][:, :, 1], EPS, None, ALU.add)\
                          .then_inc(var3_ready, 1)
                    for g in range(NG):
                        dve.wait_ge(std3_ready, NG * b + g + 1)
                        step(nc.vector.reciprocal(rstd3[g], rstd3[g]))
                        for c in range(GT):
                            last = nc.vector.tensor_scalar(xn[g][:, c, :], x2[g][:, c, :],
                                                           mean_var3[g][:, c, 0:1], rstd3[g][:, c:c + 1],
                                                           ALU.subtract, ALU.mult)
                        last.then_inc(xn_ready, 1)
                    for g in range(NG):
                        for f in range(FC):
                            dve.wait_ge(sig_ready, 2 + FC * NG * b + FC * g + f + 1)
                            nc.vector.scalar_tensor_tensor(gated[g][:, f, :], banks[:, 4 + f % 2, :],
                                                           b_1[:, f:f + 1], sig[f % 2],
                                                           ALU.add, ALU.mult).then_inc(gated_ready, 1)
                    for g in range(NG):
                        dve.wait_ge(x2_biased, NG * b + g + 1)
                        for i in range(2):
                            dve.wait_ge(down_ready, 2 * NG * b + 2 * g + i + 1)
                            nc.vector.tensor_tensor(x2[g][:, 2 * i:2 * i + 2, :],
                                                    banks[:, 6 + i, :].rearrange("p (c d) -> p c d", c=2),
                                                    x2[g][:, 2 * i:2 * i + 2, :], ALU.add).then_inc(y_ready, 1)
                    assert steps[1] == per_batch

            @block.tensor
            def _(pe):
                pe.sem_inc(ctxT_ready, NG)
                pe.wait_ge(ffn_w_in, 16 * len(ffn_loads))
                with pe.Fori(0, B) as b:
                    pe.wait_ge(ctx_in_ready, 16 * b + 16)
                    for g in range(NG):
                        for c in range(DC):
                            for i in range(GT):
                                last = nc.tensor.transpose(banks[:, c, i * P:(i + 1) * P],
                                                           ctx_in[:, g * GT + i, c * P:(c + 1) * P], ident[:, :])
                        last.then_inc(ctxT_ready, 1)
                        pe.wait_ge(ctxT_saved, DC * NG * b + DC * g + DC)
                        for i in range(2):
                            pe.wait_ge(x2_ready, 2 * NG * b + 2 * g + i + 1)
                            for j in range(2):
                                t = 2 * i + j
                                for kc in range(DC):
                                    last = nc.tensor.matmul(banks[:, 2 + i, j * D:(j + 1) * D],
                                                            ctxT[g][:, kc, t * P:(t + 1) * P], w_o[:, kc, :],
                                                            start=(kc == 0), stop=(kc == DC - 1))
                            last.then_inc(proj_ready, 1)
                    for g in range(NG):
                        pe.wait_ge(xn_ready, NG * b + g + 1)
                        for c in range(DC):
                            for i in range(GT):
                                last = nc.tensor.transpose(banks[:, c, i * P:(i + 1) * P],
                                                           xn[g][:, i, c * P:(c + 1) * P], ident[:, :])
                        last.then_inc(hT_ready, 1)
                        pe.wait_ge(hT_saved, DC * NG * b + DC * g + DC)
                        for f in range(FC):
                            pe.wait_ge(gated_ready, FC * NG * b + FC * g + f + 1)
                            for kc in range(DC):
                                last = nc.tensor.matmul(banks[:, 4 + f % 2, :], w_1[:, kc, f * P:(f + 1) * P],
                                                        hT[g][:, kc, :], start=(kc == 0), stop=(kc == DC - 1))
                            last.then_inc(up_ready, 1)
                    for g in range(NG):
                        pe.wait_ge(gated_ready, 2 + FC * NG * b + FC * g + FC)
                        for i in range(2):
                            pe.wait_ge(y_ready, 2 * NG * b + 2 * g + i + 1)
                            for j in range(2):
                                t = 2 * i + j
                                for f in range(FC):
                                    last = nc.tensor.matmul(banks[:, 6 + i, j * D:(j + 1) * D],
                                                            gated[g][:, f, t * P:(t + 1) * P], w_2[:, f, :],
                                                            start=(f == 0), stop=(f == FC - 1))
                            last.then_inc(down_ready, 1)


_INS = {
    "x": "x", "itok": "itok_B_34_63", "bias": "fside_Bx16xSxS_0", "mask": "mask_Bx1xSxS_bk0",
    "W_ada": "L0_cond_W_ada", "b_ada": "L0_cond_b_ada", "Wq": "L0_cond_Wq", "bq": "L0_cond_bq",
    "Wk": "L0_cond_Wk", "bk": "L0_cond_bk", "Wv": "L0_cond_Wv", "bv": "L0_cond_bv", "Wo": "L0_cond_Wo",
    "bo": "L0_cond_bo", "W1": "L0_cond_W1", "b1": "L0_cond_b1", "W2": "L0_cond_W2", "b2": "L0_cond_b2",
    "g2": "L0_cond_g2", "beta2": "L0_cond_beta2",
}


def kernel(**inputs):
    import concourse.bacc as bacc
    from concourse.bass_utils import run_bass_kernel_spmd

    arrays = {short: np.ascontiguousarray(inputs[name]) for short, name in _INS.items()}
    arrays["bias"] = arrays["bias"].reshape(U, S, S)
    arrays["mask"] = arrays["mask"].reshape(B, S, S)
    half = D // 2
    arrays["freqs"] = np.exp(np.arange(half, dtype=np.float32) * np.float32(-math.log(10000.0) / (half - 1)))
    arrays["ident"] = np.eye(P, dtype=np.float32)

    nc = bacc.Bacc("TRN2", target_bir_lowering=False, num_devices=1)
    aps = {n: nc.dram_tensor(f"in_{n}", v.shape, mybir.dt.from_np(v.dtype), kind="ExternalInput").ap()
           for n, v in arrays.items()}
    out = nc.dram_tensor("out_x", (B, S, D), F32, kind="ExternalOutput").ap()
    layer_kernel(nc, aps, out)
    r = run_bass_kernel_spmd(nc, [{f"in_{n}": v for n, v in arrays.items()}], core_ids=[0])
    return r.results[0]["out_x"]
```

```python
import math
from contextlib import ExitStack

import numpy as np

import concourse.bass as bass
from concourse import mybir

P = 128
B, S, D, H, F = 2, 1024, 256, 16, 1024
HD = D // H
U = B * H
T = S // P
DC = D // P
FC = F // P
GT = 4
GN = GT * P
NG = S // GN
QK = 2 * DC
VW = 32
QUADS = 4
QW = S // QUADS
PARTS = 4
PER_GROUP = 16 * (2 + 3)
EPS = 1e-5
MASKED = -3.0e38
NO_KEY = 1.5e38
PE_TILES = (2,)
DVE_MASKS = []
POOL_MASKS = [(t, half) for t in range(T) if t not in PE_TILES for half in range(2)
              if (t, half) not in [m[1:] for m in DVE_MASKS]]
ACT_TILES = ()
MAGIC = 1.5 * 2.0**23
TWO_PI_1 = 6.28125
TWO_PI_2 = round((2 * math.pi - TWO_PI_1) * 2**20) / 2**20
TWO_PI_3 = 2 * math.pi - TWO_PI_1 - TWO_PI_2
PI_BELOW = 3.1415925

F32 = mybir.dt.float32
F32R = mybir.dt.float32r
BF16 = mybir.dt.bfloat16
U8 = mybir.dt.uint8
I32 = mybir.dt.int32
ALU = mybir.AluOpType
ACT = mybir.ActivationFunctionType


def layer_kernel(nc, a, out):
    q_parts = nc.dram_tensor("q_parts", (U, 2, HD, S), F32, kind="Internal").ap()
    k_parts = nc.dram_tensor("k_parts", (U, 3, HD, S), F32, kind="Internal").ap()
    x1_dram = nc.dram_tensor("x1_dram", (B, S, D), F32, kind="Internal").ap()

    ctx = ExitStack()
    with ctx:
        def sb(name, shape, dt=F32):
            return ctx.enter_context(nc.sbuf_tensor(name, shape, dt))

        def sem(name):
            return ctx.enter_context(nc.semaphore(name))

        def wait_apart(engine, *waits):
            targets = [(semaphore, engine.to_reg(value)) for semaphore, value in waits]
            engine.wait_ge(consts_in, 16 * len(const_loads))
            for semaphore, register in targets:
                engine.wait_ge(semaphore, register)

        def as_row(name, n):
            return a[name].rearrange("(o n) -> o n", o=1).broadcast_to([P, n])

        def as_columns(name):
            return a[name].rearrange("(c p) -> p c", p=P)

        def as_chunks(name):
            return a[name].rearrange("(c p) n -> p c n", p=P)

        ident = sb("ident", [P, P])
        ident_bf = sb("ident_bf", [P, P], BF16)
        neg_mask = sb("neg_mask", [P, B, T, S], BF16)
        v_all = sb("v_all", [P, U, T, HD])
        ctx_all = sb("ctx_all", [P, B, T, D])
        ring = sb("ring", [P, T, S])
        q_st = sb("q_st", [P, 2, S], F32R)
        k_st = sb("k_st", [P, 2, S], F32R)
        v_st = sb("v_st", [P, 2, T, VW])
        big = sb("big", [P, 2, T, S])
        raw_ctx = sb("raw_ctx", [P, QW])
        neg_max = sb("neg_max", [P, 2, T])
        inv_sum = sb("inv_sum", [P, QW // P, QUADS])
        w_o = sb("w_o", [P, DC, D])
        w_1 = sb("w_1", [P, DC, F])
        w_2 = sb("w_2", [P, FC, D])
        cols = sb("cols", [P, 2 * FC + 2 * DC])
        banks = ctx.enter_context(nc.psum_tensor("banks", [P, 8, 512], F32))

        big_words = big[:, :, :, :].rearrange("p a t s -> p (a t s)")
        taken = [0]

        def carve(*shape, dt=F32):
            n = int(np.prod(shape)) // (4 if dt == U8 else 1)
            flat = big_words[:, taken[0]:taken[0] + n]
            taken[0] += n
            assert taken[0] <= 2 * T * S
            if dt != F32:
                flat = flat.bitcast(dt)
            if len(shape) == 1:
                return flat
            names = "abc"[:len(shape)]
            sizes = dict(zip(names[1:], shape[1:]))
            return flat.rearrange(f"p ({' '.join(names)}) -> p {' '.join(names)}", **sizes)

        def over(row, n):
            return row.rearrange("p (o k) -> p o k", o=1).broadcast_to([P, n, row.shape[-1]])

        x1 = ctx_all
        xT = [carve(DC, GN) for _ in range(NG)]
        qk_f32 = [carve(GN) for _ in range(2)]
        qk_parts = [carve(2, GN, dt=F32R) for _ in range(2)]
        mask_u8 = [carve(T, S, dt=U8) for _ in range(B)]
        w_q, w_k, w_v = (carve(DC, D) for _ in range(3))
        w_ada = carve(DC, 2 * D)
        b_v = carve(D)
        b_ada = carve(2 * D)
        mod = carve(B, 2 * D)
        silu_wide = carve(DC * B, P)
        small = carve(32)
        freqs, b_q, b_k, b_qs = small[:, 0:1], small[:, 1:3], small[:, 3:5], small[:, 5:7]
        t_f, t_q, t_hi, t_lo = small[:, 8:10], small[:, 10:12], small[:, 12:14], small[:, 14:16]
        angle, turns, silu, e_neg = small[:, 16:20], small[:, 20:24], small[:, 24:28], small[:, 28:32]
        stats = carve(B, T, 6)
        mean_var = carve(B, T, 2)
        rstd = carve(B, T)
        t_i = sb("t_i", [P, B], I32)
        t_bf = sb("t_bf", [P, B], BF16)

        consts_in, w_in, ffn_w_in = sem("consts_in"), sem("w_in"), sem("ffn_w_in")
        x_in_ready = [sem(f"x_in_ready{b}") for b in range(B)]
        x1_saved = sem("x1_saved")
        early_in, w_ada_in = sem("early_in"), sem("w_ada_in")
        mask_in, mask_done = [sem(f"mask_in{b}") for b in range(B)], sem("mask_done")
        angle_ready, sin_ready, en_ready = sem("angle_ready"), sem("sin_ready"), sem("en_ready")
        silu_ready, ada_ready = sem("silu_ready"), sem("ada_ready")
        var_ready, std_ready, x1_ready = sem("var_ready"), sem("std_ready"), sem("x1_ready")
        xT_ready, xT_saved = sem("xT_ready"), sem("xT_saved")
        qk_ready, qk_copied, qk_split = sem("qk_ready"), sem("qk_copied"), sem("qk_split")
        parts_saved = [sem(f"parts_saved{i}") for i in range(2)]
        v_ready, v_saved, b_qs_ready = sem("v_ready"), sem("v_saved"), sem("b_qs_ready")
        dve_step, pool_step, fixed_ready = sem("dve_step"), sem("pool_step"), sem("fixed_ready")
        bias_in = [sem(f"bias_in{t}") for t in range(T)]

        stacks_in = [sem(f"stacks_in{i}") for i in range(2)]

        def load_bias(sp, u, t):
            sp.dma_start(ring[:, t, :], a["bias"][u, t * P:(t + 1) * P, :]).then_inc(bias_in[t], 16)

        def load_stacks(sp, u, parity):
            for r in range(2):
                rows = slice(2 * HD * r, 2 * HD * (r + 1))
                for src, dst in ((q_parts[u, :, :, :], q_st), (k_parts[u, r:r + 2, :, :], k_st)):
                    sp.dma_start(dst[rows, parity, :].bitcast(F32), src.rearrange("a d s -> (a d) s"))\
                      .then_inc(stacks_in[parity], 16)

        early_loads = [(t_i[:, :], as_row("itok", B)), (freqs, a["freqs"].rearrange("(p o) -> p o", o=1))]
        const_loads = [
            (ident[:, :], a["ident"]), (b_ada, as_row("b_ada", 2 * D)), (b_q, as_columns("bq")),
            (b_k, as_columns("bk")), (b_v, as_row("bv", D)),
        ]
        b_1, b_1s = cols[:, 0:FC], cols[:, FC:2 * FC]
        g_2, beta_2 = cols[:, 2 * FC:2 * FC + DC], cols[:, 2 * FC + DC:]
        ffn_loads = [
            (w_o[:, :, :], as_chunks("Wo")), (w_1[:, :, :], as_chunks("W1")), (w_2[:, :, :], as_chunks("W2")),
            (b_1, as_columns("b1")),
            (g_2, as_columns("g2")), (beta_2, as_columns("beta2")),
        ]

        block = ctx.enter_context(nc.Block())

        @block.sync
        def _(sp):
            for dst, src in early_loads:
                sp.dma_start(dst, src, allow_slow_non_contiguous=True).then_inc(early_in, 16)
            sp.dma_start(w_ada, as_chunks("W_ada")).then_inc(w_ada_in, 16)
            for b in range(B):
                sp.dma_start(x1[:, b, :, :], a["x"][b, :, :].rearrange("(t p) d -> p t d", p=P))\
                  .then_inc(x_in_ready[b], 16)
                for dst, src in (const_loads if b == 0 else []):
                    sp.dma_start(dst, src, allow_slow_non_contiguous=True).then_inc(consts_in, 16)
            for b in range(B):
                sp.dma_start(mask_u8[b], a["mask"][b, :, :].rearrange("(t p) k -> p t k", p=P))\
                  .then_inc(mask_in[b], 16)

            def store_x1(k):
                b, g = divmod(k, NG)
                sp.wait_ge(x1_ready, k + 1)
                sp.dma_start(x1_dram[b, g * GN:(g + 1) * GN, :].rearrange("(c p) d -> p c d", p=P),
                             x1[:, b, g * GT:(g + 1) * GT, :]).then_inc(x1_saved, 16)

            store_x1(0)
            for k in range(B * NG):
                b, g = divmod(k, NG)
                if k + 1 < B * NG:
                    store_x1(k + 1)
                if k == NG:
                    for i in range(2):
                        sp.wait_ge(parts_saved[i], 32 + PER_GROUP * NG)
                    sp.wait_ge(fixed_ready, 1)
                    load_stacks(sp, 0, 0)
                    load_stacks(sp, 1, 1)
                for n in range(QK):
                    sp.wait_ge(qk_split, 2 + QK * k + n + 1)
                    dst = (q_parts, k_parts)[n // DC]
                    first_head = b * H + (n % DC) * (H // DC)
                    for part in range((2, 3)[n // DC]):
                        sp.dma_start(dst[first_head:first_head + H // DC, part, :, g * GN:(g + 1) * GN],
                                     qk_parts[n % 2][:, part % 2, :].bitcast(F32))\
                          .then_inc(parts_saved[n % 2], 16)
            for i in range(2):
                sp.wait_ge(parts_saved[i], 32 + PER_GROUP * NG * B)

        @block.gpsimd
        def _(pool):
            for w, name in ((w_q, "Wq"), (w_k, "Wk"), (w_v, "Wv")):
                pool.dma_start(w, as_chunks(name)).then_inc(w_in, 16)
            pool.memset(q_st[:, :, :].bitcast(F32), 0.0)
            pool.memset(k_st[:, :, :].bitcast(F32), 0.0)
            pool.memset(v_st[:, :, :, :], 0.0).then_inc(pool_step, 1)
            pool.wait_ge(pool_step, 1)
            pool.memset(v_st[:, :, :, HD:HD + 1], 1.0).then_inc(fixed_ready, 1)
            pool.wait_ge(consts_in, 16 * len(const_loads))
            pool.tensor_copy(ident_bf[:, :], ident[:, :]).then_inc(fixed_ready, 1)
            for dst, src in ffn_loads:
                pool.dma_start(dst, src, allow_slow_non_contiguous=True).then_inc(ffn_w_in, 16)

        @block.scalar
        def _(act):
            act.wait_ge(angle_ready, 1)
            act.activation(silu, angle, ACT.Sin).then_inc(sin_ready, 1)
            act.wait_ge(sin_ready, 1)
            act.activation(e_neg, silu, ACT.Exp, scale=-1.0).then_inc(en_ready, 1)
            act.wait_ge(var_ready, 1)
            act.activation(rstd, mean_var[:, :, :, 1], ACT.Sqrt).then_inc(std_ready, 1)
            for t in range(T):
                load_bias(act, 0, t)

            def copy_xT(k):
                act.wait_ge(xT_ready, k + 1)
                for c in range(DC):
                    act.activation(xT[k % 2][:, c, :], banks[:, c, :], ACT.Copy).then_inc(xT_saved, 1)

            copy_xT(0)
            act.wait_ge(b_qs_ready, 1)
            for k in range(B * NG):
                b, g = divmod(k, NG)
                for n in range(QK):
                    act.wait_ge(qk_ready, QK * k + n + 1)
                    act.wait_ge(qk_split, QK * k + n + 1)
                    act.activation(qk_f32[n % 2], banks[:, 2 + n % 2, :], ACT.Identity,
                                   bias=(b_qs, b_k)[n // DC][:, n % DC:n % DC + 1],
                                   scale=(HD ** -0.5, 1.0)[n // DC]).then_inc(qk_copied, 1)
                    if n == QK - 1 and k + 1 < B * NG:
                        copy_xT(k + 1)
                    if g == 0 and n == 0:
                        act.wait_ge(mask_in[b], 16)
                    t = QK * g + n
                    act.activation(neg_mask[:, b, t, :], mask_u8[b][:, t, :], ACT.Copy, scale=MASKED)\
                       .then_inc(mask_done, 1)

        @block.vector
        def _(dve):
            steps = [0]

            def step(instruction):
                instruction.then_inc(dve_step, 1)
                steps[0] += 1
                dve.wait_ge(dve_step, steps[0])

            dve.sem_inc(qk_split, 2)
            dve.sem_inc(v_saved, 2)
            for i in range(2):
                dve.sem_inc(parts_saved[i], 32)
            dve.wait_ge(early_in, 16 * len(early_loads))
            step(nc.vector.tensor_copy(t_f, t_i[:, :]))
            step(nc.vector.tensor_scalar(t_q, t_f, 0.01, None, ALU.mult))
            step(nc.vector.tensor_copy(t_bf[:, :], t_q))
            step(nc.vector.tensor_tensor(t_lo, t_q, t_bf[:, :], ALU.subtract))
            step(nc.vector.scalar_tensor_tensor(t_hi, t_bf[:, :], -100.0, t_f, ALU.mult, ALU.add))
            step(nc.vector.scalar_tensor_tensor(t_hi, t_lo, -100.0, t_hi, ALU.mult, ALU.add))
            step(nc.vector.scalar_tensor_tensor(t_q, t_hi, 0.01, t_q, ALU.mult, ALU.add))
            for c in range(DC):
                step(nc.vector.tensor_scalar(angle[:, c * B:(c + 1) * B], t_q, 4000.0, freqs,
                                             ALU.mult, ALU.mult))
            step(nc.vector.tensor_scalar(turns, angle, 1 / (2 * math.pi), None, ALU.mult))
            step(nc.vector.tensor_scalar(turns[:, B:], turns[:, B:], 0.25, None, ALU.add))
            step(nc.vector.tensor_scalar(turns, turns, MAGIC, None, ALU.add))
            step(nc.vector.tensor_scalar(turns, turns, -MAGIC, None, ALU.add))
            for part in (TWO_PI_1, TWO_PI_2, TWO_PI_3):
                step(nc.vector.scalar_tensor_tensor(angle, turns, -part, angle, ALU.mult, ALU.add))
            step(nc.vector.tensor_scalar(angle[:, B:], angle[:, B:], math.pi / 2, None, ALU.add))
            nc.vector.tensor_scalar(angle, angle, PI_BELOW, -PI_BELOW, ALU.min, ALU.max)\
              .then_inc(angle_ready, 1)

            def moments(b):
                dve.wait_ge(x_in_ready[b], 16)
                for t in range(T):
                    last = nc.vector.bn_stats(stats[:, b, t, :], x1[:, b, t, :])
                return last

            moments(0)
            dve.wait_ge(en_ready, 1)
            step(nc.vector.tensor_scalar(e_neg, e_neg, 1.0, None, ALU.add))
            step(nc.vector.reciprocal(e_neg, e_neg))
            step(nc.vector.tensor_tensor(silu, silu, e_neg, ALU.mult))
            nc.vector.tensor_copy(silu_wide, silu.rearrange("p (c o) -> p c o", o=1)
                                  .broadcast_to([P, DC * B, P])).then_inc(silu_ready, 1)
            dve.wait_ge(consts_in, 16 * len(const_loads))
            nc.vector.tensor_scalar(b_qs, b_q, HD ** -0.5, None, ALU.mult).then_inc(b_qs_ready, 1)
            step(moments(1))
            for b in range(B):
                for t in range(T):
                    last = nc.vector.bn_aggr(mean_var[:, b, t, :], stats[:, b, t, :])
            step(last)
            nc.vector.tensor_scalar(mean_var[:, :, :, 1], mean_var[:, :, :, 1], EPS, None, ALU.add)\
              .then_inc(var_ready, 1)
            for i in range(B):
                dve.wait_ge(ada_ready, i + 1)
                last = nc.vector.tensor_tensor(mod[:, i, :], banks[:, 6 + i, :], b_ada, ALU.add)
            step(last)
            step(nc.vector.tensor_scalar(mod[:, :, 0:D], mod[:, :, 0:D], 1.0, None, ALU.add))
            dve.wait_ge(std_ready, 1)
            step(nc.vector.reciprocal(rstd, rstd))

            def modulate(k):
                b, g = divmod(k, NG)
                tiles = range(g * GT, (g + 1) * GT)
                for t in tiles:
                    last = nc.vector.scalar_tensor_tensor(
                        x1[:, b, t, :], x1[:, b, t, :], mean_var[:, b, t, 0:1], mod[:, b, 0:D],
                        ALU.subtract, ALU.mult)
                step(last)
                for t in tiles:
                    last = nc.vector.scalar_tensor_tensor(
                        x1[:, b, t, :], x1[:, b, t, :], rstd[:, b, t:t + 1], mod[:, b, D:2 * D],
                        ALU.mult, ALU.add)
                last.then_inc(x1_ready, 1)

            modulate(0)
            for k in range(B * NG):
                b, g = divmod(k, NG)
                if k + 1 < B * NG:
                    modulate(k + 1)
                for n in range(QK):
                    dve.wait_ge(qk_copied, 2 + QK * k + n + 1)
                    dve.wait_ge(parts_saved[n % 2], 32 + PER_GROUP * k + 32 * (n // DC))
                    hi, lo = (qk_parts[n % 2][:, i, :] for i in range(2))
                    step(nc.vector.tensor_copy(hi, qk_f32[n % 2]))
                    nc.vector.tensor_tensor(lo, qk_f32[n % 2], hi.bitcast(F32), ALU.subtract)\
                      .then_inc(qk_split, 1)
                for i in range(2):
                    dve.wait_ge(v_ready, 2 * k + i + 1)
                    kt = g * GT + 2 * i
                    nc.vector.tensor_tensor(
                        v_all[:, b * H:(b + 1) * H, kt:kt + 2, :].rearrange("p h t d -> p t h d"),
                        banks[:, 4 + i, :].rearrange("p (t h d) -> p t h d", t=2, h=H),
                        over(b_v, 2).rearrange("p t (h d) -> p t h d", h=H),
                        ALU.add).then_inc(v_saved, 1)

        @block.tensor
        def _(pe):
            pe.sem_inc(xT_saved, DC)
            pe.sem_inc(qk_copied, 2)
            pe.wait_ge(silu_ready, 1)
            pe.wait_ge(w_ada_in, 16)
            for i in range(B):
                for c in range(DC):
                    last = nc.tensor.matmul(banks[:, 6 + i, :], silu_wide[:, c * B + i, :], w_ada[:, c, :],
                                            start=(c == 0), stop=(c == DC - 1))
                last.then_inc(ada_ready, 1)
            pe.wait_ge(consts_in, 16 * len(const_loads))
            pe.wait_ge(w_in, 16 * 3)

            def transpose_x1(k):
                b, g = divmod(k, NG)
                pe.wait_ge(x1_ready, k + 1)
                pe.wait_ge(xT_saved, DC * k + DC)
                for c in range(DC):
                    for i in range(GT):
                        last = nc.tensor.transpose(banks[:, c, i * P:(i + 1) * P],
                                                   x1[:, b, g * GT + i, c * P:(c + 1) * P], ident[:, :])
                last.then_inc(xT_ready, 1)

            transpose_x1(0)
            for k in range(B * NG):
                pe.wait_ge(xT_saved, DC * k + 2 * DC)
                for n in range(QK):
                    w, c = (w_q, w_k)[n // DC], n % DC
                    pe.wait_ge(qk_copied, QK * k + n + 1)
                    for kc in range(DC):
                        last = nc.tensor.matmul(banks[:, 2 + n % 2, :], w[:, kc, c * P:(c + 1) * P],
                                                xT[k % 2][:, kc, :], start=(kc == 0), stop=(kc == DC - 1))
                    last.then_inc(qk_ready, 1)
                if k + 1 < B * NG:
                    transpose_x1(k + 1)
                for i in range(2):
                    pe.wait_ge(v_saved, 2 * k + i + 1)
                    for j in range(2):
                        t = 2 * i + j
                        for kc in range(DC):
                            last = nc.tensor.matmul(banks[:, 4 + i, j * D:(j + 1) * D],
                                                    xT[k % 2][:, kc, t * P:(t + 1) * P], w_v[:, kc, :],
                                                    start=(kc == 0), stop=(kc == DC - 1))
                    last.then_inc(v_ready, 1)

        masked = sem("masked")
        dve_masked = sem("dve_masked")
        scores_ready = sem("scores_ready")
        shifted = sem("shifted")
        probs_ready = sem("probs_ready")
        pt_ready = [sem(f"pt_ready{i}") for i in range(2)]
        pt_saved = [sem(f"pt_saved{i}") for i in range(2)]
        v_staged = sem("v_staged")
        pv_done = sem("pv_done")
        raw_saved = sem("raw_saved")
        back_ready = sem("back_ready")
        inv_ready, ctx_stored = sem("inv_ready"), sem("ctx_stored")
        pts = [big[:, i, :, :] for i in range(2)]
        ctx_in = sb("ctx_in", [P, T, D])
        ctx_in_ready = sem("ctx_in_ready")
        LEAD = 2
        HALF = T // 2

        def head_pairs(engine, first, end, emit):
            assert first % 2 == 0 and end % 2 == 0
            with engine.Fori(0, (end - first) // 2) as i:
                for parity in range(2):
                    emit(2 * i + first + parity, parity)


        @block.sync
        def _(sp):
            def head(u, parity):
                for t in range(T):
                    sp.wait_ge(pt_ready[1], T + T * u - T + t + 1)
                    load_bias(sp, u, t)
                    if t == 2:
                        sp.wait_ge(scores_ready, T * u - T)
                        load_stacks(sp, u, parity)

            for t in range(T):
                sp.wait_ge(pt_ready[1], T + t + 1)
                load_bias(sp, 1, t)
            head_pairs(sp, 2, U, head)
            sp.wait_ge(ctx_stored, 1 + H)
            sp.dma_start(ctx_in[:, :, :], ctx_all[:, 0, :, :]).then_inc(ctx_in_ready, 16)

        @block.gpsimd
        def _(pool):
            def head(u, parity):
                for t in range(T):
                    halves = [half for tile, half in POOL_MASKS if tile == t]
                    if not halves:
                        continue
                    keys = slice(halves[0] * S // 2, (halves[-1] + 1) * S // 2)
                    pool.wait_ge(bias_in[t], 16 * u + 16)
                    pool.tensor_tensor(
                        ring[:, t, keys], ring[:, t, keys],
                        neg_mask[:, bass.ds(u // H, 1), t, keys].rearrange("p o k -> p (o k)"),
                        ALU.add).then_inc(masked, len(halves))

            pool.wait_ge(mask_done, T)
            head_pairs(pool, 0, H, head)
            pool.wait_ge(mask_done, T * B)
            head_pairs(pool, H, U, head)

        @block.vector
        def _(dve):
            def normalise(u):
                back = banks[:, 7, 0:QW].rearrange("p (i j w) -> p i j w", i=QW // P, j=QUADS)
                dve.wait_ge(back_ready, u + 2)
                nc.vector.reciprocal(inv_sum[:, :, :], back[:, :, :, HD]).then_inc(inv_ready, 1)
                dve.wait_ge(inv_ready, u + 1)
                dst = ctx_all[:, bass.ds(u // H, 1), :, bass.ds((u % H) * HD, HD)]\
                    .rearrange("p o (j i) d -> p (o i) j d", i=QW // P)
                nc.vector.tensor_tensor(
                    dst, back[:, :, :, 0:HD],
                    inv_sum[:, :, :].rearrange("p i (j o) -> p i j o", o=1)
                    .broadcast_to([P, QW // P, QUADS, HD]),
                    ALU.mult).then_inc(ctx_stored, 1)

            def shift(u, parity, t):
                s = 2 * (t % 2)
                waits = [(scores_ready, T * u + t + 1)]
                if t in PE_TILES:
                    waits.append((bias_in[t], 16 * u + 16))
                for semaphore, masks in ((masked, POOL_MASKS), (dve_masked, [m[1:] for m in DVE_MASKS])):
                    mine = [i for i, m in enumerate(masks) if m[0] == t]
                    if mine:
                        waits.append((semaphore, len(masks) * u + mine[-1] + 1))
                wait_apart(dve, *waits)
                nc.vector.tensor_tensor_reduce(
                    out=ring[:, t, :], in0=banks[:, s:s + 2, :].rearrange("p b n -> p (b n)"),
                    in1=ring[:, t, :], scale=-1.0, scalar=NO_KEY, op0=ALU.add, op1=ALU.min,
                    accum_out=neg_max[:, parity, t:t + 1]).then_inc(shifted, 1)

            def head(u, parity, normalises=True, ahead=True):
                for t in range(T):
                    if t == 0:
                        dve.wait_ge(pv_done, u + 1)
                    if t == 4 and normalises:
                        normalise(u - 2)
                    if t + LEAD < T:
                        shift(u, parity, t + LEAD)
                    elif ahead:
                        shift(u + 1, 1 - parity, t + LEAD - T)
                    if t not in ACT_TILES:
                        dve.wait_ge(pt_ready[1], T + T * u + t + 1)
                        nc.vector.tensor_copy(pts[parity][:, HALF:T, t * P:(t + 1) * P],
                                              banks[:, 5, :].rearrange("p (k q) -> p k q", k=HALF))\
                          .then_inc(pt_saved[1], 1)
                    for step, tile, half in DVE_MASKS:
                        if step == t:
                            keys = slice(half * S // 2, (half + 1) * S // 2)
                            dve.wait_ge(bias_in[tile], 16 * u + 16)
                            nc.vector.tensor_tensor(
                                ring[:, tile, keys], ring[:, tile, keys],
                                neg_mask[:, bass.ds(u // H, 1), tile, keys].rearrange("p o k -> p (o k)"),
                                ALU.add).then_inc(dve_masked, 1)

            dve.wait_ge(x1_saved, 16 * NG * B)
            dve.sem_inc(ctx_stored, 1)
            dve.sem_inc(shifted, LEAD)
            for t in range(LEAD):
                shift(0, 0, t)
            head(0, 0, normalises=False)
            head(1, 1, normalises=False)
            head_pairs(dve, 2, U - 2, head)
            head(U - 2, 0)
            head(U - 1, 1, ahead=False)
            normalise(U - 2)
            normalise(U - 1)

        @block.scalar
        def _(act):
            def save_raw(u):
                act.wait_ge(pv_done, u + 3)
                act.wait_ge(back_ready, u + 1)
                act.activation(raw_ctx[:, :], banks[:, 6, 0:QW], ACT.Copy).then_inc(raw_saved, 1)

            def exponentials(u, parity, t):
                act.wait_ge(shifted, LEAD + T * u + t + 1)
                act.activation(ring[:, t, :], ring[:, t, :], ACT.Exp, scale=-1.0,
                               bias=neg_max[:, parity, t:t + 1]).then_inc(probs_ready, 1)

            def head(u, parity, saves=True, ahead=True):
                for t in range(T):
                    if t + 1 < T:
                        exponentials(u, parity, t + 1)
                    elif ahead:
                        exponentials(u + 1, 1 - parity, 0)
                    if t == 0:
                        act.wait_ge(pv_done, u + 1)
                        if saves:
                            save_raw(u - 2)
                    if t == 4:
                        act.activation(
                            v_st[:, parity, :, 0:HD],
                            v_all[:, bass.ds(u, 1), :, :].rearrange("p o t d -> p (o t) d"),
                            ACT.Copy).then_inc(v_staged, 1)
                    for half in range(2 if t in ACT_TILES else 1):
                        act.wait_ge(pt_ready[half], T * half + T * u + t + 1)
                        act.activation(pts[parity][:, half * HALF:(half + 1) * HALF, t * P:(t + 1) * P],
                                       banks[:, 4 + half, :].rearrange("p (k q) -> p k q", k=HALF),
                                       ACT.Copy).then_inc(pt_saved[half], 1)

            act.sem_inc(raw_saved, 1)
            for i in range(2):
                act.sem_inc(pt_saved[i], 1)
            exponentials(0, 0, 0)
            head(0, 0, saves=False)
            head(1, 1, saves=False)
            head_pairs(act, 2, U - 2, head)
            head(U - 2, 0)
            head(U - 1, 1, ahead=False)
            save_raw(U - 2)
            save_raw(U - 1)

        @block.tensor
        def _(pe):
            def scores(u, parity, t):
                s = 2 * (t % 2)
                if t == 0:
                    pe.wait_ge(stacks_in[parity], 64 * (u // 2) + 64)
                pe.wait_ge(shifted, T * u + t + 1)
                for c in range(S // 512):
                    by_pe = t in PE_TILES
                    last = nc.tensor.matmul(banks[:, s + c, :], q_st[:, parity, t * P:(t + 1) * P],
                                            k_st[:, parity, c * 512:(c + 1) * 512],
                                            start=True, stop=not by_pe)
                    if by_pe:
                        mask = neg_mask[:, bass.ds(u // H, 1), t, c * 512:(c + 1) * 512]
                        last = nc.tensor.matmul(banks[:, s + c, :], ident_bf[:, :],
                                                mask.rearrange("p o k -> p (o k)"), start=False, stop=True)
                last.then_inc(scores_ready, 1)

            def transposes(u, t):
                pe.wait_ge(probs_ready, T * u + t + 1)
                for half in range(2):
                    pe.wait_ge(pt_saved[half], T * u + t + 1)
                    for k in range(HALF):
                        kt = half * HALF + k
                        last = nc.tensor.transpose(banks[:, 4 + half, k * P:(k + 1) * P],
                                                   ring[:, t, kt * P:(kt + 1) * P], ident[:, :])
                    last.then_inc(pt_ready[half], 1)

            def values(u, parity, kt):
                if kt == 0:
                    for half in range(2):
                        pe.wait_ge(pt_saved[half], T * u + T + 1)
                    pe.wait_ge(v_staged, u + 1)
                    pe.wait_ge(raw_saved, u + 1)
                for j in range(QUADS):
                    last = nc.tensor.matmul(banks[VW * j:VW * (j + 1), 6, 0:QW], v_st[:, parity, kt, :],
                                            pts[parity][:, kt, j * QW:(j + 1) * QW],
                                            start=(kt == 0), stop=(kt == T - 1))
                if kt == T - 1:
                    last.then_inc(pv_done, 1)

            def back(u):
                pe.wait_ge(raw_saved, u + 2)
                pe.wait_ge(ctx_stored, u + 1)
                for i in range(QW // P):
                    last = nc.tensor.transpose(banks[:, 7, i * P:(i + 1) * P],
                                               raw_ctx[:, i * P:(i + 1) * P], ident[:, :])
                last.then_inc(back_ready, 1)

            def head(u, parity, ahead=True, before=1):
                for t in range(T):
                    if t + LEAD < T:
                        scores(u, parity, t + LEAD)
                    elif ahead:
                        scores(u + 1, 1 - parity, t + LEAD - T)
                    transposes(u, t)
                    if t == 1 and before >= 2:
                        back(u - 2)
                    if before >= 1:
                        values(u - 1, 1 - parity, t)

            pe.sem_inc(pt_ready[1], T)
            pe.sem_inc(pv_done, 2)
            pe.sem_inc(back_ready, 1)
            pe.wait_ge(xT_saved, DC + DC * NG * B)
            pe.wait_ge(qk_copied, 2 + QK * NG * B)
            scores(0, 0, 0)
            scores(0, 0, 1)
            pe.wait_ge(v_saved, 2 + 2 * NG * B)
            pe.wait_ge(fixed_ready, 2)
            pe.wait_ge(mask_done, T * B)
            for i in range(2):
                pe.wait_ge(parts_saved[i], 32 + PER_GROUP * NG * B)
            head(0, 0, before=0)
            head(1, 1, before=1)
            head_pairs(pe, 2, U - 2, lambda u, parity: head(u, parity, before=2))
            head(U - 2, 0, before=2)
            head(U - 1, 1, ahead=False, before=2)
            back(U - 2)
            for kt in range(T):
                values(U - 1, 1, kt)
            back(U - 1)

        taken[0] = 0
        x2 = v_all[:, :, :, :].rearrange("p u t d -> p (u t d)").rearrange("p (b t d) -> p b t d", b=B, t=T)
        xn = [carve(GT, D) for _ in range(NG)]
        ctxT = [carve(DC, GN) for _ in range(NG)]
        hT = [carve(DC, GN) for _ in range(NG)]
        b_o, b_2 = carve(D), carve(D)
        assert taken[0] <= T * S
        taken[0] = T * S
        gated = [carve(FC, GN) for _ in range(NG)]
        rows_in = sem("rows_in")
        sig = [ring[:, i, 0:GN] for i in range(2)]
        stats3 = ring[:, 2, 0:6 * B * T].rearrange("p (c k) -> p c k", k=6)
        mean_var3 = ring[:, 3, 0:2 * B * T].rearrange("p (b t k) -> p b t k", b=B, t=T)
        rstd3 = ring[:, 3, 512:512 + B * T].rearrange("p (b t) -> p b t", b=B)

        x1_back = [sem(f"x1_back{b}") for b in range(B)]
        ctxT_ready, ctxT_saved = sem("ctxT_ready"), sem("ctxT_saved")
        x1_biased, proj_ready, x2_ready = sem("x1_biased"), sem("proj_ready"), sem("x2_ready")
        var3_ready, std3_ready, xn_ready = sem("var3_ready"), sem("std3_ready"), sem("xn_ready")
        hT_ready, hT_saved = sem("hT_ready"), sem("hT_saved")
        up_ready, sig_ready, gated_ready = sem("up_ready"), sem("sig_ready"), sem("gated_ready")
        down_ready, x2_biased, y_ready = sem("down_ready"), sem("x2_biased"), sem("y_ready")
        stored, dve_step3, b_1s_ready = sem("stored"), sem("dve_step3"), sem("b_1s_ready")

        def tile_rows(dram, b):
            return dram[b, :, :].rearrange("(t p) d -> p t d", p=P)

        def of_batch(tensor, b, first, n):
            return tensor[:, bass.ds(b, 1), first:first + n, :].rearrange("p o t d -> p (o t) d")


        @block.sync
        def _(sp):
            sp.wait_ge(pv_done, 2 + U - 1)
            for dst, name in ((b_o, "bo"), (b_2, "b2")):
                sp.dma_start(dst, as_row(name, D)).then_inc(rows_in, 16)
            sp.wait_ge(x1_saved, 16 * NG * B)
            sp.wait_ge(v_staged, U)
            for b in range(B):
                sp.dma_start(x2[:, b, :, :], tile_rows(x1_dram, b)).then_inc(x1_back[b], 16)
            sp.wait_ge(ctxT_ready, NG)
            sp.wait_ge(ctx_stored, 1 + U)
            sp.dma_start(ctx_in[:, :, :], ctx_all[:, 1, :, :]).then_inc(ctx_in_ready, 16)
            with sp.Fori(0, B) as b:
                for g in range(NG):
                    sp.wait_ge(y_ready, 2 + 2 * NG * b + 2 * g + 2)
                    sp.dma_start(out[b, g * GN:(g + 1) * GN, :].rearrange("(c p) d -> p c d", p=P),
                                 of_batch(x2, b, g * GT, GT)).then_inc(stored, 16)
            sp.wait_ge(stored, 16 * B * NG)

        @block.gpsimd
        def _(pool):
            pool.wait_ge(rows_in, 32)
            for b in range(B):
                pool.wait_ge(x1_back[b], 16)
                for g in range(NG):
                    x2_g = x2[:, b, g * GT:(g + 1) * GT, :]
                    pool.tensor_tensor(x2_g, x2_g, over(b_o, GT), ALU.add).then_inc(x1_biased, 1)
            with pool.Fori(0, B) as b:
                for g in range(NG):
                    x2_g = of_batch(x2, b, g * GT, GT)
                    pool.wait_ge(xn_ready, NG * b + g + 1)
                    pool.tensor_tensor(x2_g, x2_g, over(b_2, GT), ALU.add).then_inc(x2_biased, 1)

        @block.scalar
        def _(act):
            with act.Fori(0, B) as b:
                for g in range(NG):
                    act.wait_ge(ctxT_ready, NG * b + g + 1)
                    for c in range(DC):
                        act.activation(ctxT[g][:, c, :], banks[:, 2 * g + c, :], ACT.Copy)\
                           .then_inc(ctxT_saved, 1)
            act.wait_ge(var3_ready, 1)
            act.activation(rstd3, mean_var3[:, :, :, 1], ACT.Sqrt).then_inc(std3_ready, 1)
            act.wait_ge(b_1s_ready, 1)
            act.sem_inc(sig_ready, 2)
            with act.Fori(0, B) as b:
                for g in range(NG):
                    act.wait_ge(hT_ready, NG + NG * b + g + 1)
                    for c in range(DC):
                        act.activation(hT[g][:, c, :], banks[:, 2 * g + c, :], ACT.Identity,
                                       scale=g_2[:, c:c + 1], bias=beta_2[:, c:c + 1]).then_inc(hT_saved, 1)
                for g in range(NG):
                    for f in range(FC):
                        n = FC * NG * b + FC * g + f
                        act.wait_ge(up_ready, n + 1)
                        act.wait_ge(gated_ready, n + 1)
                        act.activation(sig[f % 2], banks[:, 4 + f % 2, :], ACT.Sigmoid, scale=1.702,
                                       bias=b_1s[:, f:f + 1]).then_inc(sig_ready, 1)

        @block.vector
        def _(dve):
            dve.sem_inc(gated_ready, 2)
            dve.sem_inc(x2_ready, 4)
            dve.sem_inc(y_ready, 2)
            dve.wait_ge(ffn_w_in, 16 * len(ffn_loads))
            nc.vector.tensor_scalar(b_1s, b_1, 1.702, None, ALU.mult).then_inc(b_1s_ready, 1)
            for b in range(B):
                for g in range(NG):
                    dve.wait_ge(x1_biased, NG * b + g + 1)
                    for i in range(2):
                        dve.wait_ge(proj_ready, 2 * NG * b + 2 * g + i + 1)
                        pair = x2[:, b, g * GT + 2 * i:g * GT + 2 * i + 2, :]
                        nc.vector.tensor_tensor(
                            pair, banks[:, 4 + 2 * g + i, :].rearrange("p (c d) -> p c d", c=2), pair,
                            ALU.add).then_inc(x2_ready, 1)
                    dve.wait_ge(x2_ready, 4 + 2 * NG * b + 2 * g + 2)
                    for t in range(g * GT, (g + 1) * GT):
                        last = nc.vector.bn_stats(stats3[:, b * T + t, :], x2[:, b, t, :])
            last.then_inc(dve_step3, 1)
            dve.wait_ge(dve_step3, 1)
            for b in range(B):
                for t in range(T):
                    last = nc.vector.bn_aggr(mean_var3[:, b, t, :], stats3[:, b * T + t, :])
            last.then_inc(dve_step3, 1)
            dve.wait_ge(dve_step3, 2)
            nc.vector.tensor_scalar(mean_var3[:, :, :, 1], mean_var3[:, :, :, 1], EPS, None, ALU.add)\
              .then_inc(var3_ready, 1)
            dve.wait_ge(std3_ready, 1)
            nc.vector.reciprocal(rstd3, rstd3).then_inc(dve_step3, 1)
            dve.wait_ge(dve_step3, 3)
            with dve.Fori(0, B) as b:
                for g in range(NG):
                    dve.wait_ge(hT_ready, NG * b + g + 1)
                    for c in range(GT):
                        t = g * GT + c
                        last = nc.vector.tensor_scalar(
                            xn[g][:, c, :], of_batch(x2, b, t, 1).rearrange("p t d -> p (t d)"),
                            of_batch(mean_var3, b, t, 1)[:, :, 0:1].rearrange("p t k -> p (t k)"),
                            rstd3[:, bass.ds(b, 1), t:t + 1].rearrange("p o k -> p (o k)"),
                            ALU.subtract, ALU.mult)
                    last.then_inc(xn_ready, 1)
                for g in range(NG):
                    for f in range(FC):
                        dve.wait_ge(sig_ready, 2 + FC * NG * b + FC * g + f + 1)
                        nc.vector.scalar_tensor_tensor(gated[g][:, f, :], banks[:, 4 + f % 2, :],
                                                       b_1[:, f:f + 1], sig[f % 2],
                                                       ALU.add, ALU.mult).then_inc(gated_ready, 1)
                for g in range(NG):
                    dve.wait_ge(x2_biased, NG * b + g + 1)
                    for i in range(2):
                        dve.wait_ge(down_ready, 2 * NG * b + 2 * g + i + 1)
                        pair = of_batch(x2, b, g * GT + 2 * i, 2)
                        nc.vector.tensor_tensor(
                            pair, banks[:, 6 + i, :].rearrange("p (c d) -> p c d", c=2), pair,
                            ALU.add).then_inc(y_ready, 1)

        @block.tensor
        def _(pe):
            pe.wait_ge(ffn_w_in, 16 * len(ffn_loads))
            pe.wait_ge(shifted, LEAD + T * U)
            pe.wait_ge(raw_saved, 1 + U)
            pe.wait_ge(ctx_stored, 1 + U)
            with pe.Fori(0, B) as b:
                pe.wait_ge(ctx_in_ready, 16 * b + 16)
                for g in range(NG):
                    for c in range(DC):
                        for i in range(GT):
                            last = nc.tensor.transpose(banks[:, 2 * g + c, i * P:(i + 1) * P],
                                                       ctx_in[:, g * GT + i, c * P:(c + 1) * P], ident[:, :])
                    last.then_inc(ctxT_ready, 1)
                for g in range(NG):
                    pe.wait_ge(ctxT_saved, DC * NG * b + DC * g + DC)
                    for i in range(2):
                        pe.wait_ge(x2_ready, 2 * NG * b + 2 * g + i + 1)
                        for j in range(2):
                            t = 2 * i + j
                            for kc in range(DC):
                                last = nc.tensor.matmul(banks[:, 4 + 2 * g + i, j * D:(j + 1) * D],
                                                        ctxT[g][:, kc, t * P:(t + 1) * P], w_o[:, kc, :],
                                                        start=(kc == 0), stop=(kc == DC - 1))
                        last.then_inc(proj_ready, 1)
            pe.sem_inc(hT_ready, NG)
            pe.wait_ge(x2_ready, 4 + 2 * NG * B)
            with pe.Fori(0, B) as b:
                for g in range(NG):
                    pe.wait_ge(xn_ready, NG * b + g + 1)
                    for c in range(DC):
                        for i in range(GT):
                            last = nc.tensor.transpose(banks[:, 2 * g + c, i * P:(i + 1) * P],
                                                       xn[g][:, i, c * P:(c + 1) * P], ident[:, :])
                    last.then_inc(hT_ready, 1)
                for g in range(NG):
                    pe.wait_ge(hT_saved, DC * NG * b + DC * g + DC)
                    for f in range(FC):
                        pe.wait_ge(gated_ready, FC * NG * b + FC * g + f + 1)
                        for kc in range(DC):
                            last = nc.tensor.matmul(banks[:, 4 + f % 2, :], w_1[:, kc, f * P:(f + 1) * P],
                                                    hT[g][:, kc, :], start=(kc == 0), stop=(kc == DC - 1))
                        last.then_inc(up_ready, 1)
                for g in range(NG):
                    pe.wait_ge(gated_ready, 2 + FC * NG * b + FC * g + FC)
                    for i in range(2):
                        pe.wait_ge(y_ready, 2 * NG * b + 2 * g + i + 1)
                        for j in range(2):
                            t = 2 * i + j
                            for f in range(FC):
                                last = nc.tensor.matmul(banks[:, 6 + i, j * D:(j + 1) * D],
                                                        gated[g][:, f, t * P:(t + 1) * P], w_2[:, f, :],
                                                        start=(f == 0), stop=(f == FC - 1))
                        last.then_inc(down_ready, 1)


_INS = {
    "x": "x", "itok": "itok_B_34_63", "bias": "fside_Bx16xSxS_0", "mask": "mask_Bx1xSxS_bk0",
    "W_ada": "L0_cond_W_ada", "b_ada": "L0_cond_b_ada", "Wq": "L0_cond_Wq", "bq": "L0_cond_bq",
    "Wk": "L0_cond_Wk", "bk": "L0_cond_bk", "Wv": "L0_cond_Wv", "bv": "L0_cond_bv", "Wo": "L0_cond_Wo",
    "bo": "L0_cond_bo", "W1": "L0_cond_W1", "b1": "L0_cond_b1", "W2": "L0_cond_W2", "b2": "L0_cond_b2",
    "g2": "L0_cond_g2", "beta2": "L0_cond_beta2",
}


def kernel(**inputs):
    import concourse.bacc as bacc
    from concourse.bass_utils import run_bass_kernel_spmd

    arrays = {short: np.ascontiguousarray(inputs[name]) for short, name in _INS.items()}
    arrays["bias"] = arrays["bias"].reshape(U, S, S)
    arrays["mask"] = arrays["mask"].reshape(B, S, S)
    half = D // 2
    arrays["freqs"] = np.exp(np.arange(half, dtype=np.float32) * np.float32(-math.log(10000.0) / (half - 1)))
    arrays["ident"] = np.eye(P, dtype=np.float32)

    nc = bacc.Bacc("TRN2", target_bir_lowering=False, num_devices=1)
    aps = {n: nc.dram_tensor(f"in_{n}", v.shape, mybir.dt.from_np(v.dtype), kind="ExternalInput").ap()
           for n, v in arrays.items()}
    out = nc.dram_tensor("out_x", (B, S, D), F32, kind="ExternalOutput").ap()
    layer_kernel(nc, aps, out)
    r = run_bass_kernel_spmd(nc, [{f"in_{n}": v for n, v in arrays.items()}], core_ids=[0])
    return r.results[0]["out_x"]
```

```python
import math
from contextlib import ExitStack

import numpy as np

import concourse.bass as bass
from concourse import mybir

P = 128
B, S, D, H, F = 2, 1024, 256, 16, 1024
HD = D // H
U = B * H
T = S // P
DC = D // P
FC = F // P
GT = 4
GN = GT * P
NG = S // GN
MASKS_BESIDE = -(-B * S // P // (B * NG - 1))
QK = 2 * DC
LEAD = 2
VW = 32
QUADS = 4
QW = S // QUADS
STORED = (2, 3)
STAGED = 4
EPS = 1e-5
MASKED = -3.0e38
NO_KEY = 1.5e38
DVE_MASKS = [(0, 6, 0), (2, 6, 1)]
POOL_MASKS = [(t, half) for t in range(T) for half in range(2)
              if (t, half) not in [m[1:] for m in DVE_MASKS]]
ACT_TILES = [m[0] for m in DVE_MASKS]
MAGIC = 1.5 * 2.0**23
TWO_PI_1 = 6.28125
TWO_PI_2 = round((2 * math.pi - TWO_PI_1) * 2**20) / 2**20
TWO_PI_3 = 2 * math.pi - TWO_PI_1 - TWO_PI_2
PI_BELOW = 3.1415925

F32 = mybir.dt.float32
F32R = mybir.dt.float32r
BF16 = mybir.dt.bfloat16
U8 = mybir.dt.uint8
I32 = mybir.dt.int32
ALU = mybir.AluOpType
ACT = mybir.ActivationFunctionType


def layer_kernel(nc, a, out):
    q_parts = nc.dram_tensor("q_parts", (U, 2, HD, S), F32, kind="Internal").ap()
    k_parts = nc.dram_tensor("k_parts", (U, 3, HD, S), F32, kind="Internal").ap()
    x1_dram = nc.dram_tensor("x1_dram", (B, S, D), F32, kind="Internal").ap()

    ctx = ExitStack()
    with ctx:
        def sb(name, shape, dt=F32):
            return ctx.enter_context(nc.sbuf_tensor(name, shape, dt))

        def sem(name):
            return ctx.enter_context(nc.semaphore(name))

        def wait_apart(engine, *waits):
            targets = [(semaphore, engine.to_reg(value)) for semaphore, value in waits]
            engine.wait_ge(consts_in, 16 * len(const_loads))
            for semaphore, register in targets:
                engine.wait_ge(semaphore, register)

        def as_row(name, n):
            return a[name].rearrange("(o n) -> o n", o=1).broadcast_to([P, n])

        def as_columns(name):
            return a[name].rearrange("(c p) -> p c", p=P)

        def as_chunks(name):
            return a[name].rearrange("(c p) n -> p c n", p=P)

        early = ctx.enter_context(ExitStack())

        def early_sb(name, shape, dt=F32):
            return early.enter_context(nc.sbuf_tensor(name, shape, dt))

        ident = sb("ident", [P, P])
        v_all = sb("v_all", [P, U, T, HD])
        ctx_all = sb("ctx_all", [P, B, T, D])
        q_st = sb("q_st", [P, 2, S], F32R)
        k_st = sb("k_st", [P, 2, S], F32R)
        v_st = sb("v_st", [P, 2, T, VW])
        raw_ctx = sb("raw_ctx", [P, QW])
        neg_max = sb("neg_max", [P, 2, T])
        inv_sum = sb("inv_sum", [P, QW // P, QUADS])
        cols = sb("cols", [P, 2 * FC + 2 * DC])
        t_i, t_bf = sb("t_i", [P, B], I32), sb("t_bf", [P, B], BF16)
        w_o = early_sb("w_o", [P, DC, D])
        w_1 = early_sb("w_1", [P, DC, F])
        w_2 = early_sb("w_2", [P, FC, D])
        neg_mask = early_sb("neg_mask", [P, B, T, S], BF16)
        ring = early_sb("ring", [P, T, S])
        big = early_sb("big", [P, 2, T, S])
        banks = ctx.enter_context(nc.psum_tensor("banks", [P, 8, 512], F32))

        big_words = big[:, :, :, :].rearrange("p a t s -> p (a t s)")
        taken = [0]

        def carve(*shape, dt=F32):
            n = int(np.prod(shape)) // (4 if dt == U8 else 1)
            flat = big_words[:, taken[0]:taken[0] + n]
            taken[0] += n
            assert taken[0] <= 2 * T * S
            if dt != F32:
                flat = flat.bitcast(dt)
            if len(shape) == 1:
                return flat
            names = "abc"[:len(shape)]
            sizes = dict(zip(names[1:], shape[1:]))
            return flat.rearrange(f"p ({' '.join(names)}) -> p {' '.join(names)}", **sizes)

        def over(row, n):
            return row.rearrange("p (o k) -> p o k", o=1).broadcast_to([P, n, row.shape[-1]])

        x1 = ctx_all
        mask_u8 = [carve(T, S, dt=U8) for _ in range(B)]
        w_q, w_k, w_v = (carve(DC, D) for _ in range(3))
        w_ada = carve(DC, 2 * D)
        mod = carve(B, 2 * D)
        silu_wide = carve(DC * B, P)
        assert taken[0] == T * S
        qk_parts = [carve(2, GN, dt=F32R) for _ in range(QK)]
        xT = [carve(DC, GN) for _ in range(NG)]
        qk_f32 = [carve(GN) for _ in range(2)]
        b_v = carve(D)
        b_ada = carve(2 * D)
        small = carve(32)
        freqs, b_q, b_k, b_qs = small[:, 0:1], small[:, 1:3], small[:, 3:5], small[:, 5:7]
        t_f, t_q, t_hi, t_lo = small[:, 8:10], small[:, 10:12], small[:, 12:14], small[:, 14:16]
        angle, turns, silu, e_neg = small[:, 16:20], small[:, 20:24], small[:, 24:28], small[:, 28:32]
        stats = carve(B, T, 6)
        mean_var = carve(B, T, 2)
        rstd = carve(B, T)

        consts_in, w_in, ffn_w_in = sem("consts_in"), sem("w_in"), sem("ffn_w_in")
        x_in_ready = [sem(f"x_in_ready{b}") for b in range(B)]
        x1_saved = sem("x1_saved")
        early_in, w_ada_in = sem("early_in"), sem("w_ada_in")
        mask_in, mask_done = [sem(f"mask_in{b}") for b in range(B)], sem("mask_done")
        angle_ready, sin_ready, en_ready = sem("angle_ready"), sem("sin_ready"), sem("en_ready")
        silu_ready, ada_ready = sem("silu_ready"), sem("ada_ready")
        var_ready, std_ready, x1_ready = sem("var_ready"), sem("std_ready"), sem("x1_ready")
        xT_ready, xT_saved = sem("xT_ready"), sem("xT_saved")
        qk_ready, qk_copied, qk_split = sem("qk_ready"), sem("qk_copied"), sem("qk_split")
        parts_saved = [sem(f"parts_saved{i}") for i in range(QK)]
        v_ready, v_saved, b_qs_ready = sem("v_ready"), sem("v_saved"), sem("b_qs_ready")
        dve_step, pool_step, fixed_ready = sem("dve_step"), sem("pool_step"), sem("fixed_ready")
        bias_in = [sem(f"bias_in{t}") for t in range(T)]

        shifted = sem("shifted")
        stacks_in = [sem(f"stacks_in{i}") for i in range(2)]

        def load_bias(sp, u, t):
            sp.dma_start(ring[:, t, :], a["bias"][u, t * P:(t + 1) * P, :]).then_inc(bias_in[t], 16)

        def load_stacks(sp, u, parity):
            for r in range(2):
                rows = slice(2 * HD * r, 2 * HD * (r + 1))
                for src, dst in ((q_parts[u, :, :, :], q_st), (k_parts[u, r:r + 2, :, :], k_st)):
                    sp.dma_start(dst[rows, parity, :].bitcast(F32), src.rearrange("a d s -> (a d) s"))\
                      .then_inc(stacks_in[parity], 16)

        def stored_parts(n, groups):
            return 16 * STORED[n // DC] * (1 + groups)

        early_loads = [(t_i[:, :], as_row("itok", B)), (freqs, a["freqs"].rearrange("(p o) -> p o", o=1))]
        const_loads = [
            (ident[:, :], a["ident"]), (b_ada, as_row("b_ada", 2 * D)), (b_q, as_columns("bq")),
            (b_k, as_columns("bk")), (b_v, as_row("bv", D)),
        ]
        b_1, b_1s = cols[:, 0:FC], cols[:, FC:2 * FC]
        g_2, beta_2 = cols[:, 2 * FC:2 * FC + DC], cols[:, 2 * FC + DC:]
        ffn_loads = [
            (w_o[:, :, :], as_chunks("Wo")), (w_1[:, :, :], as_chunks("W1")), (w_2[:, :, :], as_chunks("W2")),
            (b_1, as_columns("b1")),
            (g_2, as_columns("g2")), (beta_2, as_columns("beta2")),
        ]

        def project_v(pe, k):
            for i in range(2):
                pe.wait_ge(v_saved, 2 * k + i + 1)
                for j in range(2):
                    t = 2 * i + j
                    for kc in range(DC):
                        last = nc.tensor.matmul(banks[:, 4 + i, j * D:(j + 1) * D],
                                                xT[k % 2][:, kc, t * P:(t + 1) * P], w_v[:, kc, :],
                                                start=(kc == 0), stop=(kc == DC - 1))
                last.then_inc(v_ready, 1)

        def save_v(dve, k):
            b, g = divmod(k, NG)
            for i in range(2):
                dve.wait_ge(v_ready, 2 * k + i + 1)
                kt = g * GT + 2 * i
                nc.vector.tensor_tensor(
                    v_all[:, b * H:(b + 1) * H, kt:kt + 2, :].rearrange("p h t d -> p t h d"),
                    banks[:, 4 + i, :].rearrange("p (t h d) -> p t h d", t=2, h=H),
                    over(b_v, 2).rearrange("p t (h d) -> p t h d", h=H),
                    ALU.add).then_inc(v_saved, 1)

        block = ctx.enter_context(nc.Block())

        @block.sync
        def _(sp):
            for dst, src in early_loads:
                sp.dma_start(dst, src, allow_slow_non_contiguous=True).then_inc(early_in, 16)
            sp.dma_start(w_ada, as_chunks("W_ada")).then_inc(w_ada_in, 16)
            for b in range(B):
                sp.dma_start(x1[:, b, :, :], a["x"][b, :, :].rearrange("(t p) d -> p t d", p=P))\
                  .then_inc(x_in_ready[b], 16)
                for dst, src in (const_loads if b == 0 else []):
                    sp.dma_start(dst, src, allow_slow_non_contiguous=True).then_inc(consts_in, 16)
            for b in range(B):
                sp.dma_start(mask_u8[b], a["mask"][b, :, :].rearrange("(t p) k -> p t k", p=P))\
                  .then_inc(mask_in[b], 16)

            def store_x1(k):
                b, g = divmod(k, NG)
                sp.wait_ge(x1_ready, k + 1)
                sp.dma_start(x1_dram[b, g * GN:(g + 1) * GN, :].rearrange("(c p) d -> p c d", p=P),
                             x1[:, b, g * GT:(g + 1) * GT, :]).then_inc(x1_saved, 16)

            store_x1(0)
            for k in range(B * NG):
                b, g = divmod(k, NG)
                if k + 1 < B * NG:
                    store_x1(k + 1)
                if k == NG:
                    for n in range(QK):
                        sp.wait_ge(parts_saved[n], stored_parts(n, NG))
                    sp.wait_ge(fixed_ready, 1)
                    load_stacks(sp, 0, 0)
                    load_stacks(sp, 1, 1)
                for n in range(QK):
                    sp.wait_ge(qk_split, 2 + QK * k + n + 1)
                    dst = (q_parts, k_parts)[n // DC]
                    first_head = b * H + (n % DC) * (H // DC)
                    for part in range(STORED[n // DC]):
                        sp.dma_start(dst[first_head:first_head + H // DC, part, :, g * GN:(g + 1) * GN],
                                     qk_parts[n][:, part % 2, :].bitcast(F32))\
                          .then_inc(parts_saved[n], 16)

        @block.gpsimd
        def _(pool):
            for w, name in ((w_q, "Wq"), (w_k, "Wk"), (w_v, "Wv")):
                pool.dma_start(w, as_chunks(name)).then_inc(w_in, 16)
            pool.memset(q_st[:, :, :].bitcast(F32), 0.0)
            pool.memset(k_st[:, :, :].bitcast(F32), 0.0)
            pool.memset(v_st[:, :, :, :], 0.0).then_inc(pool_step, 1)
            pool.wait_ge(pool_step, 1)
            pool.memset(v_st[:, :, :, HD:HD + 1], 1.0).then_inc(fixed_ready, 1)
            for dst, src in ffn_loads:
                pool.dma_start(dst, src, allow_slow_non_contiguous=True).then_inc(ffn_w_in, 16)

        @block.scalar
        def _(act):
            act.wait_ge(angle_ready, 1)
            act.activation(silu, angle, ACT.Sin).then_inc(sin_ready, 1)
            act.wait_ge(sin_ready, 1)
            act.activation(e_neg, silu, ACT.Exp, scale=-1.0).then_inc(en_ready, 1)

            def deviation(b):
                act.wait_ge(var_ready, b + 1)
                act.activation(rstd[:, b, :], mean_var[:, b, :, 1], ACT.Sqrt).then_inc(std_ready, 1)

            deviation(0)
            for t in range(T):
                load_bias(act, 0, t)

            def copy_xT(k):
                act.wait_ge(xT_ready, k + 1)
                for c in range(DC):
                    act.activation(xT[k % 2][:, c, :], banks[:, c, :], ACT.Copy).then_inc(xT_saved, 1)

            def convert_mask(first, end):
                for i in range(first, min(end, T * B)):
                    if i % T == 0:
                        act.wait_ge(mask_in[i // T], 16)
                    act.activation(neg_mask[:, i // T, i % T, :], mask_u8[i // T][:, i % T, :], ACT.Copy,
                                   scale=MASKED).then_inc(mask_done, 1)

            copy_xT(0)
            act.wait_ge(b_qs_ready, 1)
            for k in range(B * NG):
                b, g = divmod(k, NG)
                for n in range(QK):
                    act.wait_ge(qk_ready, QK * k + n + 1)
                    act.wait_ge(qk_split, QK * k + n + 1)
                    act.activation(qk_f32[n % 2], banks[:, 2 + n % 2, :], ACT.Identity,
                                   bias=(b_qs, b_k)[n // DC][:, n % DC:n % DC + 1],
                                   scale=(HD ** -0.5, 1.0)[n // DC]).then_inc(qk_copied, 1)
                    convert_mask(MASKS_BESIDE * k + n, MASKS_BESIDE * k + n + 1)
                if g == 0 and b + 1 < B:
                    deviation(b + 1)
                if k + 1 < B * NG:
                    copy_xT(k + 1)
                convert_mask(MASKS_BESIDE * k + QK, MASKS_BESIDE * (k + 1))
                if k == B * NG - 2:
                    act.activation(e_neg, e_neg, ACT.Exp)

        @block.vector
        def _(dve):
            steps = [0]

            def step(instruction):
                instruction.then_inc(dve_step, 1)
                steps[0] += 1
                dve.wait_ge(dve_step, steps[0])

            dve.sem_inc(qk_split, 2)
            dve.sem_inc(v_saved, 2)
            dve.sem_inc(shifted, LEAD)
            for n in range(QK):
                dve.sem_inc(parts_saved[n], stored_parts(n, 0))
            dve.wait_ge(early_in, 16 * len(early_loads))
            step(nc.vector.tensor_copy(t_f, t_i[:, :]))
            step(nc.vector.tensor_scalar(t_q, t_f, 0.01, None, ALU.mult))
            step(nc.vector.tensor_copy(t_bf[:, :], t_q))
            step(nc.vector.tensor_tensor(t_lo, t_q, t_bf[:, :], ALU.subtract))
            step(nc.vector.scalar_tensor_tensor(t_hi, t_bf[:, :], -100.0, t_f, ALU.mult, ALU.add))
            step(nc.vector.scalar_tensor_tensor(t_hi, t_lo, -100.0, t_hi, ALU.mult, ALU.add))
            step(nc.vector.scalar_tensor_tensor(t_q, t_hi, 0.01, t_q, ALU.mult, ALU.add))
            for c in range(DC):
                step(nc.vector.tensor_scalar(angle[:, c * B:(c + 1) * B], t_q, 4000.0, freqs,
                                             ALU.mult, ALU.mult))
            step(nc.vector.tensor_scalar(turns, angle, 1 / (2 * math.pi), None, ALU.mult))
            step(nc.vector.tensor_scalar(turns[:, B:], turns[:, B:], 0.25, None, ALU.add))
            step(nc.vector.tensor_scalar(turns, turns, MAGIC, None, ALU.add))
            step(nc.vector.tensor_scalar(turns, turns, -MAGIC, None, ALU.add))
            for part in (TWO_PI_1, TWO_PI_2, TWO_PI_3):
                step(nc.vector.scalar_tensor_tensor(angle, turns, -part, angle, ALU.mult, ALU.add))
            step(nc.vector.tensor_scalar(angle[:, B:], angle[:, B:], math.pi / 2, None, ALU.add))
            nc.vector.tensor_scalar(angle, angle, PI_BELOW, -PI_BELOW, ALU.min, ALU.max)\
              .then_inc(angle_ready, 1)

            def moments(b):
                dve.wait_ge(x_in_ready[b], 16)
                for t in range(T):
                    last = nc.vector.bn_stats(stats[:, b, t, :], x1[:, b, t, :])
                return last

            def variance(b):
                step(moments(b))
                for t in range(T):
                    last = nc.vector.bn_aggr(mean_var[:, b, t, :], stats[:, b, t, :])
                step(last)
                nc.vector.tensor_scalar(mean_var[:, b, :, 1], mean_var[:, b, :, 1], EPS, None, ALU.add)\
                  .then_inc(var_ready, 1)

            dve.wait_ge(en_ready, 1)
            step(nc.vector.tensor_scalar(e_neg, e_neg, 1.0, None, ALU.add))
            step(nc.vector.reciprocal(e_neg, e_neg))
            step(nc.vector.tensor_tensor(silu, silu, e_neg, ALU.mult))
            nc.vector.tensor_copy(silu_wide, silu.rearrange("p (c o) -> p c o", o=1)
                                  .broadcast_to([P, DC * B, P])).then_inc(silu_ready, 1)
            dve.wait_ge(consts_in, 16 * len(const_loads))
            nc.vector.tensor_scalar(b_qs, b_q, HD ** -0.5, None, ALU.mult).then_inc(b_qs_ready, 1)
            variance(0)

            def modulate(k):
                b, g = divmod(k, NG)
                tiles = range(g * GT, (g + 1) * GT)
                if g == 0:
                    dve.wait_ge(std_ready, b + 1)
                    step(nc.vector.reciprocal(rstd[:, b, :], rstd[:, b, :]))
                    dve.wait_ge(ada_ready, b + 1)
                    step(nc.vector.tensor_tensor(mod[:, b, :], banks[:, 6 + b, :], b_ada, ALU.add))
                    step(nc.vector.tensor_scalar(mod[:, b, 0:D], mod[:, b, 0:D], 1.0, None, ALU.add))
                for t in tiles:
                    last = nc.vector.scalar_tensor_tensor(
                        x1[:, b, t, :], x1[:, b, t, :], mean_var[:, b, t, 0:1], mod[:, b, 0:D],
                        ALU.subtract, ALU.mult)
                step(last)
                for t in tiles:
                    last = nc.vector.scalar_tensor_tensor(
                        x1[:, b, t, :], x1[:, b, t, :], rstd[:, b, t:t + 1], mod[:, b, D:2 * D],
                        ALU.mult, ALU.add)
                last.then_inc(x1_ready, 1)

            modulate(0)
            for k in range(B * NG):
                b, g = divmod(k, NG)
                if g == 0 and b + 1 < B:
                    variance(b + 1)
                if k + 1 < B * NG:
                    modulate(k + 1)
                for n in range(QK):
                    dve.wait_ge(qk_copied, 2 + QK * k + n + 1)
                    dve.wait_ge(parts_saved[n], stored_parts(n, k))
                    hi, lo = (qk_parts[n][:, i, :] for i in range(2))
                    step(nc.vector.tensor_copy(hi, qk_f32[n % 2]))
                    nc.vector.tensor_tensor(lo, qk_f32[n % 2], hi.bitcast(F32), ALU.subtract)\
                      .then_inc(qk_split, 1)
                if k + 1 < B * NG:
                    save_v(dve, k)

        @block.tensor
        def _(pe):
            pe.sem_inc(xT_saved, DC)
            pe.sem_inc(qk_copied, 2)
            pe.wait_ge(silu_ready, 1)
            pe.wait_ge(w_ada_in, 16)
            for i in range(B):
                for c in range(DC):
                    last = nc.tensor.matmul(banks[:, 6 + i, :], silu_wide[:, c * B + i, :], w_ada[:, c, :],
                                            start=(c == 0), stop=(c == DC - 1))
                last.then_inc(ada_ready, 1)
            pe.wait_ge(consts_in, 16 * len(const_loads))

            def transpose_x1(k):
                b, g = divmod(k, NG)
                pe.wait_ge(x1_ready, k + 1)
                pe.wait_ge(xT_saved, DC * k + DC)
                for c in range(DC):
                    for i in range(GT):
                        last = nc.tensor.transpose(banks[:, c, i * P:(i + 1) * P],
                                                   x1[:, b, g * GT + i, c * P:(c + 1) * P], ident[:, :])
                last.then_inc(xT_ready, 1)

            transpose_x1(0)
            pe.wait_ge(w_in, 16 * 3)
            for k in range(B * NG):
                for n in range(QK):
                    w, c = (w_q, w_k)[n // DC], n % DC
                    pe.wait_ge(qk_copied, QK * k + n + 1)
                    for kc in range(DC):
                        if n == 0:
                            pe.wait_ge(xT_saved, DC + DC * k + kc + 1)
                        last = nc.tensor.matmul(banks[:, 2 + n % 2, :], w[:, kc, c * P:(c + 1) * P],
                                                xT[k % 2][:, kc, :], start=(kc == 0), stop=(kc == DC - 1))
                    last.then_inc(qk_ready, 1)
                if k + 1 < B * NG:
                    transpose_x1(k + 1)
                    project_v(pe, k)

        masked = sem("masked")
        dve_masked = sem("dve_masked")
        scores_ready = sem("scores_ready")
        probs_ready = sem("probs_ready")
        pt_ready = [sem(f"pt_ready{i}") for i in range(2)]
        pt_saved = [sem(f"pt_saved{i}") for i in range(2)]
        v_staged = sem("v_staged")
        pv_done = sem("pv_done")
        raw_saved = sem("raw_saved")
        back_ready = sem("back_ready")
        inv_ready, ctx_stored = sem("inv_ready"), sem("ctx_stored")
        pts = [big[:, i, :, :] for i in range(2)]
        HALF = T // 2

        ctxT_ready = sem("ctxT_ready")
        out_back = banks[:, 7, 0:QW].rearrange("p (i j w) -> p i j w", i=QW // P, j=QUADS)

        def save_raw(act, u):
            act.wait_ge(pv_done, u + 3)
            act.wait_ge(back_ready, u + 1)
            act.activation(raw_ctx[:, :], banks[:, 6, 0:QW], ACT.Copy).then_inc(raw_saved, 1)

        def back(pe, u):
            pe.wait_ge(raw_saved, u + 2)
            pe.wait_ge(ctx_stored, u + 1)
            for i in range(QW // P):
                last = nc.tensor.transpose(banks[:, 7, i * P:(i + 1) * P],
                                           raw_ctx[:, i * P:(i + 1) * P], ident[:, :])
            last.then_inc(back_ready, 1)

        def invert_sums(dve, u):
            dve.wait_ge(back_ready, u + 2)
            nc.vector.reciprocal(inv_sum[:, :, :], out_back[:, :, :, HD]).then_inc(inv_ready, 1)

        def normalise(dve, u):
            dve.wait_ge(inv_ready, u + 1)
            dst = ctx_all[:, bass.ds(u // H, 1), :, bass.ds((u % H) * HD, HD)]\
                .rearrange("p o (j i) d -> p (o i) j d", i=QW // P)
            nc.vector.tensor_tensor(
                dst, out_back[:, :, :, 0:HD],
                inv_sum[:, :, :].rearrange("p i (j o) -> p i j o", o=1)
                .broadcast_to([P, QW // P, QUADS, HD]),
                ALU.mult).then_inc(ctx_stored, 1)

        def transpose_ctx(pe, k):
            b, g = divmod(k, NG)
            for c in range(DC):
                for i in range(GT):
                    last = nc.tensor.transpose(banks[:, DC * g + c, i * P:(i + 1) * P],
                                               ctx_all[:, b, g * GT + i, c * P:(c + 1) * P], ident[:, :])
            last.then_inc(ctxT_ready, 1)

        def head_pairs(engine, first, end, emit):
            assert first % 2 == 0 and end % 2 == 0
            with engine.Fori(0, (end - first) // 2) as i:
                for parity in range(2):
                    emit(2 * i + first + parity, parity)

        @block.sync
        def _(sp):
            def head(u, parity):
                for t in range(T):
                    sp.wait_ge(pt_ready[1], T + T * u - T + t + 1)
                    load_bias(sp, u, t)
                    if t == 2:
                        sp.wait_ge(scores_ready, T * u - T)
                        load_stacks(sp, u, parity)

            for t in range(T):
                sp.wait_ge(pt_ready[1], T + t + 1)
                load_bias(sp, 1, t)
            for n in range(QK):
                sp.wait_ge(parts_saved[n], stored_parts(n, NG * B))
            head_pairs(sp, 2, U, head)

        @block.gpsimd
        def _(pool):
            def head(u, parity):
                for t in range(T):
                    halves = [half for tile, half in POOL_MASKS if tile == t]
                    if not halves:
                        continue
                    keys = slice(halves[0] * S // 2, (halves[-1] + 1) * S // 2)
                    pool.wait_ge(bias_in[t], 16 * u + 16)
                    pool.tensor_tensor(
                        ring[:, t, keys], ring[:, t, keys],
                        neg_mask[:, bass.ds(u // H, 1), t, keys].rearrange("p o k -> p (o k)"),
                        ALU.add).then_inc(masked, len(halves))

            pool.wait_ge(mask_done, T)
            head_pairs(pool, 0, H, head)
            pool.wait_ge(mask_done, T * B)
            head_pairs(pool, H, U, head)

        @block.vector
        def _(dve):
            def shift(u, parity, t):
                s = 2 * (t % 2)
                waits = [(scores_ready, T * u + t + 1)]
                for semaphore, masks in ((masked, POOL_MASKS), (dve_masked, [m[1:] for m in DVE_MASKS])):
                    mine = [i for i, m in enumerate(masks) if m[0] == t]
                    if mine:
                        waits.append((semaphore, len(masks) * u + mine[-1] + 1))
                wait_apart(dve, *waits)
                nc.vector.tensor_tensor_reduce(
                    out=ring[:, t, :], in0=banks[:, s:s + 2, :].rearrange("p b n -> p (b n)"),
                    in1=ring[:, t, :], scale=-1.0, scalar=NO_KEY, op0=ALU.add, op1=ALU.min,
                    accum_out=neg_max[:, parity, t:t + 1]).then_inc(shifted, 1)

            def head(u, parity, normalises=True, ahead=True):
                for t in range(T):
                    if t == 0:
                        dve.wait_ge(pv_done, u + 1)
                    if t + LEAD < T:
                        shift(u, parity, t + LEAD)
                    elif ahead:
                        shift(u + 1, 1 - parity, t + LEAD - T)
                    if t not in ACT_TILES:
                        dve.wait_ge(pt_ready[1], T + T * u + t + 1)
                        nc.vector.tensor_copy(pts[parity][:, HALF:T, t * P:(t + 1) * P],
                                              banks[:, 5, :].rearrange("p (k q) -> p k q", k=HALF))\
                          .then_inc(pt_saved[1], 1)
                    if t == 4 and normalises:
                        invert_sums(dve, u - 2)
                    if t == 5 and normalises:
                        normalise(dve, u - 2)
                    for step, tile, half in DVE_MASKS:
                        if step == t:
                            keys = slice(half * S // 2, (half + 1) * S // 2)
                            dve.wait_ge(bias_in[tile], 16 * u + 16)
                            nc.vector.tensor_tensor(
                                ring[:, tile, keys], ring[:, tile, keys],
                                neg_mask[:, bass.ds(u // H, 1), tile, keys].rearrange("p o k -> p (o k)"),
                                ALU.add).then_inc(dve_masked, 1)

            dve.wait_ge(x1_saved, 16 * NG * B)
            dve.sem_inc(ctx_stored, 1)
            for t in range(LEAD):
                shift(0, 0, t)
            save_v(dve, B * NG - 1)
            head(0, 0, normalises=False)
            head(1, 1, normalises=False)
            head_pairs(dve, 2, U - 2, head)
            head(U - 2, 0)
            head(U - 1, 1, ahead=False)
            invert_sums(dve, U - 2)
            normalise(dve, U - 2)

        @block.scalar
        def _(act):
            def exponentials(u, parity, t):
                act.wait_ge(shifted, LEAD + T * u + t + 1)
                act.activation(ring[:, t, :], ring[:, t, :], ACT.Exp, scale=-1.0,
                               bias=neg_max[:, parity, t:t + 1]).then_inc(probs_ready, 1)

            def head(u, parity, saves=True, ahead=True):
                for t in range(T):
                    if t + 1 < T:
                        exponentials(u, parity, t + 1)
                    elif ahead:
                        exponentials(u + 1, 1 - parity, 0)
                    if t == 0:
                        act.wait_ge(pv_done, u + 1)
                        if saves:
                            save_raw(act, u - 2)
                    if t == 4:
                        act.activation(
                            v_st[:, parity, :, 0:HD],
                            v_all[:, bass.ds(u, 1), :, :].rearrange("p o t d -> p (o t) d"),
                            ACT.Copy).then_inc(v_staged, 1)
                    for half in range(2 if t in ACT_TILES else 1):
                        act.wait_ge(pt_ready[half], T * half + T * u + t + 1)
                        act.activation(pts[parity][:, half * HALF:(half + 1) * HALF, t * P:(t + 1) * P],
                                       banks[:, 4 + half, :].rearrange("p (k q) -> p k q", k=HALF),
                                       ACT.Copy).then_inc(pt_saved[half], 1)

            act.sem_inc(raw_saved, 1)
            for i in range(2):
                act.sem_inc(pt_saved[i], 1)
            exponentials(0, 0, 0)
            head(0, 0, saves=False)
            head(1, 1, saves=False)
            head_pairs(act, 2, U - 2, head)
            head(U - 2, 0)
            head(U - 1, 1, ahead=False)
            save_raw(act, U - 2)

        @block.tensor
        def _(pe):
            def scores(u, parity, t):
                s = 2 * (t % 2)
                if t == 0:
                    pe.wait_ge(stacks_in[parity], 64 * (u // 2) + 64)
                pe.wait_ge(shifted, T * u + t + 1)
                for c in range(S // 512):
                    last = nc.tensor.matmul(banks[:, s + c, :], q_st[:, parity, t * P:(t + 1) * P],
                                            k_st[:, parity, c * 512:(c + 1) * 512], start=True, stop=True)
                last.then_inc(scores_ready, 1)

            def transposes(u, t):
                pe.wait_ge(probs_ready, T * u + t + 1)
                for half in range(2):
                    pe.wait_ge(pt_saved[half], T * u + t + 1)
                    for k in range(HALF):
                        kt = half * HALF + k
                        last = nc.tensor.transpose(banks[:, 4 + half, k * P:(k + 1) * P],
                                                   ring[:, t, kt * P:(kt + 1) * P], ident[:, :])
                    last.then_inc(pt_ready[half], 1)

            def values(u, parity, kt):
                if kt == 0:
                    for half in range(2):
                        pe.wait_ge(pt_saved[half], T * u + T + 1)
                    pe.wait_ge(v_staged, u + 1)
                    pe.wait_ge(raw_saved, u + 1)
                for j in range(QUADS):
                    last = nc.tensor.matmul(banks[VW * j:VW * (j + 1), 6, 0:QW], v_st[:, parity, kt, :],
                                            pts[parity][:, kt, j * QW:(j + 1) * QW],
                                            start=(kt == 0), stop=(kt == T - 1))
                if kt == T - 1:
                    last.then_inc(pv_done, 1)

            def head(u, parity, ahead=True, before=1):
                for t in range(T):
                    if t + LEAD < T:
                        scores(u, parity, t + LEAD)
                    elif ahead:
                        scores(u + 1, 1 - parity, t + LEAD - T)
                    transposes(u, t)
                    if t == 1 and before >= 2:
                        back(pe, u - 2)
                    if before >= 1:
                        values(u - 1, 1 - parity, t)

            pe.sem_inc(pt_ready[1], T)
            pe.sem_inc(pv_done, 2)
            pe.sem_inc(back_ready, 1)
            pe.wait_ge(xT_saved, DC + DC * NG * B)
            scores(0, 0, 0)
            pe.wait_ge(qk_copied, 2 + QK * NG * B)
            scores(0, 0, 1)
            project_v(pe, B * NG - 1)
            pe.wait_ge(v_saved, 2 + 2 * NG * B)
            pe.wait_ge(fixed_ready, 1)
            head(0, 0, before=0)
            for n in range(QK):
                pe.wait_ge(parts_saved[n], stored_parts(n, NG * B))
            head(1, 1, before=1)
            head_pairs(pe, 2, U - 2, lambda u, parity: head(u, parity, before=2))
            head(U - 2, 0, before=2)
            head(U - 1, 1, ahead=False, before=2)
            back(pe, U - 2)
            pe.wait_ge(shifted, LEAD + T * U)
            pe.wait_ge(ctx_stored, 1 + H)
            for k in range(NG):
                transpose_ctx(pe, k)
            for kt in range(T):
                values(U - 1, 1, kt)

        early.close()
        gated_1 = [sb(f"gated_1_{part}", [P, FC, GN], F32R) for part in ("hi", "lo")]
        w_1_hi, w_2_hi = sb("w_1_hi", [P, DC, F], F32R), sb("w_2_hi", [P, FC, D], F32R)
        w_o_hi, w_o_lo = sb("w_o_hi", [P, DC, D], F32R), sb("w_o_lo", [P, DC, D], F32R)
        w_1_lo, w_2_lo = sb("w_1_lo", [P, DC, F], F32R), sb("w_2_lo", [P, FC, D], F32R)
        sig = sb("sig", [P, 2, GN])
        unsplit = sb("unsplit", [P, STAGED, GN])
        spare = sb("spare", [P, GN])
        hT_hi, hT_lo = (sb(f"hT_{part}", [P, B, NG * DC, GN], F32R) for part in ("hi", "lo"))
        gated_0 = [sb(f"gated_0_{part}", [P, FC, GN], F32R) for part in ("hi", "lo")]
        b_o, b_2 = sb("b_o", [P, D])[:, :], sb("b_2", [P, D])[:, :]
        stats3, mean_var3 = sb("stats3", [P, B * T, 6]), sb("mean_var3", [P, B * T, 2])
        rstd3, shift3 = sb("rstd3", [P, B * T]), sb("shift3", [P, B * T])
        gated_hi, gated_lo = zip(gated_0, gated_1)
        ctxT_hi = q_st[:, :, :].rearrange("p a (c n) -> p (a c) n", n=GN)
        ctxT_lo = k_st[:, :, :].rearrange("p a (c n) -> p (a c) n", n=GN)
        x2 = v_all[:, :, :, :].rearrange("p u t d -> p (u t d)").rearrange("p (b t d) -> p b t d", b=B, t=T)
        xn = ctx_all

        rows_in = sem("rows_in")
        x1_back = [sem(f"x1_back{b}") for b in range(B)]
        w_hi_ready, w_o_split, w_1_split, w_2_split = (sem(n) for n in ("w_hi_ready", "w_o_split", "w_1_split",
                                                                        "w_2_split"))
        ctxT_hi_ready, ctxT_lo_ready = sem("ctxT_hi_ready"), sem("ctxT_lo_ready")
        x1_biased, proj_ready, x2_ready = sem("x1_biased"), sem("proj_ready"), sem("x2_ready")
        var3_ready, std3_ready, shift3_ready = sem("var3_ready"), sem("std3_ready"), sem("shift3_ready")
        xn_ready = sem("xn_ready")
        hT_ready, hT_saved, hT_split = sem("hT_ready"), sem("hT_saved"), sem("hT_split")
        up_ready, sig_ready, gated_ready = sem("up_ready"), sem("sig_ready"), sem("gated_ready")
        gated_hi_ready, gated_split = sem("gated_hi_ready"), sem("gated_split")
        down_ready, x2_biased, y_ready = sem("down_ready"), sem("x2_biased"), sem("y_ready")
        stored, dve_step3, b_1s_ready = sem("stored"), sem("dve_step3"), sem("b_1s_ready")
        GROUPS = B * NG
        UP_BANKS = 4
        EXACT = ((0, 0), (0, 1), (1, 0))

        def of_batch(tensor, b, first, n):
            return tensor[:, bass.ds(b, 1), first:first + n, :].rearrange("p o t d -> p (o t) d")

        @block.sync
        def _(sp):
            sp.wait_ge(x1_saved, 16 * NG * B)
            for b in range(B):
                sp.wait_ge(v_staged, H * (b + 1))
                sp.dma_start(x2[:, b, :, :], x1_dram[b, :, :].rearrange("(t p) d -> p t d", p=P))\
                  .then_inc(x1_back[b], 16)
            sp.wait_ge(scores_ready, T * U)
            sp.wait_ge(masked, len(POOL_MASKS) * U)
            for dst, name in ((b_o, "bo"), (b_2, "b2")):
                sp.dma_start(dst, as_row(name, D)).then_inc(rows_in, 16)
            with sp.Fori(0, B) as b:
                for g in range(NG):
                    sp.wait_ge(y_ready, 2 + 2 * NG * b + 2 * g + 2)
                    sp.dma_start(out[b, g * GN:(g + 1) * GN, :].rearrange("(c p) d -> p c d", p=P),
                                 of_batch(x2, b, g * GT, GT)).then_inc(stored, 16)
            sp.wait_ge(stored, 16 * B * NG)

        @block.gpsimd
        def _(pool):
            pool.wait_ge(rows_in, 2 * 16)

            def add_rows(k, row, done):
                x2_g = x2[:, k // NG, (k % NG) * GT:(k % NG + 1) * GT, :]
                pool.tensor_tensor(x2_g, x2_g, over(row, GT), ALU.add).then_inc(done, 1)

            for k in range(GROUPS):
                pool.wait_ge(x1_back[k // NG], 16)
                add_rows(k, b_o, x1_biased)
            pool.wait_ge(pt_ready[1], T + T * U)
            pool.wait_ge(w_hi_ready, 2)
            pool.tensor_tensor(w_1_lo[:, :, :], w_1[:, :, :], w_1_hi[:, :, :].bitcast(F32), ALU.subtract)\
                .then_inc(w_1_split, 1)
            pool.wait_ge(w_hi_ready, 3)
            pool.tensor_tensor(w_2_lo[:, :, :], w_2[:, :, :], w_2_hi[:, :, :].bitcast(F32), ALU.subtract)\
                .then_inc(w_2_split, 1)
            for k in range(GROUPS):
                pool.wait_ge(xn_ready, k + 1)
                add_rows(k, b_2, x2_biased)
            pool.sem_inc(gated_split, STAGED)
            with pool.Fori(0, B) as b:
                for g in range(NG):
                    for f in range(FC):
                        pool.wait_ge(gated_hi_ready, FC * NG * b + FC * g + f + 1)
                        pool.tensor_tensor(gated_lo[g][:, f, :], unsplit[:, f % STAGED, :],
                                           gated_hi[g][:, f, :].bitcast(F32), ALU.subtract)\
                            .then_inc(gated_split, 1)

        @block.scalar
        def _(act):
            act.wait_ge(ffn_w_in, 16 * len(ffn_loads))
            act.wait_ge(masked, len(POOL_MASKS) * U)
            act.wait_ge(scores_ready, T * U)
            act.activation(w_o_hi[:, :, :], w_o[:, :, :], ACT.Copy).then_inc(w_hi_ready, 1)

            def copy_ctxT(k):
                act.wait_ge(ctxT_ready, k + 1)
                for c in range(DC):
                    i = DC * (k % NG) + c
                    act.activation(ctxT_hi[:, i, :], banks[:, i, :], ACT.Copy).then_inc(ctxT_hi_ready, 1)

            def normalise_x2(k):
                b, g = divmod(k, NG)
                tiles = range(GT * k, GT * (k + 1))
                act.wait_ge(var3_ready, k + 1)
                act.activation(rstd3[:, tiles[0]:tiles[-1] + 1], mean_var3[:, tiles[0]:tiles[-1] + 1, 1],
                               ACT.Sqrt).then_inc(std3_ready, 1)
                act.wait_ge(shift3_ready, k + 1)
                for t in tiles:
                    last = act.activation(xn[:, b, t - b * T, :], x2[:, b, t - b * T, :], ACT.Identity,
                                          scale=rstd3[:, t:t + 1], bias=shift3[:, t:t + 1])
                last.then_inc(xn_ready, 1)

            def copy_hT(k):
                act.wait_ge(hT_ready, k + 1)
                for c in range(DC):
                    i = DC * (k % NG) + c
                    if k > 0:
                        act.wait_ge(hT_split, DC * (k - 1) + c + 1)
                    for dst in (unsplit[:, c, :], hT_hi[:, k // NG, i, :]):
                        last = act.activation(dst, banks[:, 4 * (k // NG) + i, :], ACT.Identity,
                                              scale=g_2[:, c:c + 1], bias=beta_2[:, c:c + 1])
                    last.then_inc(hT_saved, 1)

            def split_weight(hi, w):
                act.activation(hi[:, :, :], w[:, :, :], ACT.Copy).then_inc(w_hi_ready, 1)

            act.activation(rstd3[:, 0:1], ident[:, 0:1], ACT.Sqrt)
            copy_ctxT(0)
            copy_ctxT(1)
            save_raw(act, U - 1)
            split_weight(w_1_hi, w_1)
            copy_ctxT(2)
            normalise_x2(0)
            copy_ctxT(3)
            split_weight(w_2_hi, w_2)
            normalise_x2(1)
            copy_hT(0)
            normalise_x2(2)
            copy_hT(1)
            normalise_x2(3)
            act.activation(sig[:, 0, 0:1], ident[:, 0:1], ACT.Sigmoid)
            copy_hT(2)
            copy_hT(3)
            act.wait_ge(b_1s_ready, 1)
            act.sem_inc(sig_ready, 2)
            with act.Fori(0, B) as b:
                for n in range(NG * FC + 1):
                    done = FC * NG * b + n
                    if n < NG * FC:
                        act.wait_ge(up_ready, done + 1)
                        act.wait_ge(gated_ready, UP_BANKS + done - 2 + 1)
                        act.activation(sig[:, n % 2, :], banks[:, n % UP_BANKS, :], ACT.Sigmoid, scale=1.702,
                                       bias=b_1s[:, n % FC:n % FC + 1]).then_inc(sig_ready, 1)
                    if n > 0:
                        g, f = divmod(n - 1, FC)
                        act.wait_ge(gated_ready, UP_BANKS + done)
                        act.activation(gated_hi[g][:, f, :], unsplit[:, f % STAGED, :], ACT.Copy)\
                           .then_inc(gated_hi_ready, 1)

        @block.vector
        def _(dve):
            steps = [0]

            def step(instruction):
                instruction.then_inc(dve_step3, 1)
                steps[0] += 1
                dve.wait_ge(dve_step3, steps[0])

            def split_ctxT(k):
                for c in range(DC):
                    i = DC * (k % NG) + c
                    dve.wait_ge(ctxT_hi_ready, DC * k + c + 1)
                    nc.vector.tensor_tensor(ctxT_lo[:, i, :], banks[:, i, :], ctxT_hi[:, i, :].bitcast(F32),
                                            ALU.subtract).then_inc(ctxT_lo_ready, 1)

            def add_and_norm(k):
                b, g = divmod(k, NG)
                dve.wait_ge(x1_biased, k + 1)
                for i in range(2):
                    dve.wait_ge(proj_ready, 2 * k + i + 1)
                    pair = x2[:, b, g * GT + 2 * i:g * GT + 2 * i + 2, :]
                    nc.vector.tensor_tensor(
                        pair, banks[:, 4 + 2 * g + i, :].rearrange("p (c d) -> p c d", c=2), pair,
                        ALU.add).then_inc(x2_ready, 1)
                    dve.wait_ge(x2_ready, 4 + 2 * k + i + 1)
                    for c in range(2):
                        t = g * GT + 2 * i + c
                        last = nc.vector.bn_stats(stats3[:, b * T + t, :], x2[:, b, t, :])
                step(last)
                tiles = range(b * T + g * GT, b * T + (g + 1) * GT)
                for t in tiles:
                    last = nc.vector.bn_aggr(mean_var3[:, t, :], stats3[:, t, :])
                step(last)
                variance = mean_var3[:, tiles[0]:tiles[-1] + 1, 1]
                nc.vector.tensor_scalar(variance, variance, EPS, None, ALU.add).then_inc(var3_ready, 1)
                dve.wait_ge(std3_ready, k + 1)
                root = rstd3[:, tiles[0]:tiles[-1] + 1]
                step(nc.vector.reciprocal(root, root))
                nc.vector.scalar_tensor_tensor(shift3[:, tiles[0]:tiles[-1] + 1],
                                               mean_var3[:, tiles[0]:tiles[-1] + 1, 0], -1.0, root,
                                               ALU.mult, ALU.mult).then_inc(shift3_ready, 1)

            dve.sem_inc(gated_ready, UP_BANKS)
            dve.sem_inc(x2_ready, 4)
            dve.sem_inc(y_ready, 2)
            dve.wait_ge(w_hi_ready, 1)
            nc.vector.tensor_tensor(w_o_lo[:, :, :], w_o[:, :, :], w_o_hi[:, :, :].bitcast(F32), ALU.subtract)\
              .then_inc(w_o_split, 1)
            def split_hT(k):
                for c in range(DC):
                    i = DC * (k % NG) + c
                    dve.wait_ge(hT_saved, DC * k + c + 1)
                    nc.vector.tensor_tensor(hT_lo[:, k // NG, i, :], unsplit[:, c, :],
                                            hT_hi[:, k // NG, i, :].bitcast(F32), ALU.subtract)\
                      .then_inc(hT_split, 1)

            split_ctxT(0)
            split_ctxT(1)
            invert_sums(dve, U - 1)
            normalise(dve, U - 1)
            nc.vector.tensor_scalar(b_1s, b_1, 1.702, None, ALU.mult).then_inc(b_1s_ready, 1)
            add_and_norm(0)
            split_ctxT(2)
            add_and_norm(1)
            split_ctxT(3)
            add_and_norm(2)
            split_hT(0)
            add_and_norm(3)
            split_hT(1)
            split_hT(2)
            split_hT(3)
            dve.wait_ge(hT_split, DC * GROUPS)
            with dve.Fori(0, B) as b:
                for g in range(NG):
                    for f in range(FC):
                        n = FC * NG * b + FC * g + f
                        dve.wait_ge(gated_split, n + 1)
                        dve.wait_ge(sig_ready, 2 + n + 1)
                        nc.vector.scalar_tensor_tensor(unsplit[:, f % STAGED, :], banks[:, f % UP_BANKS, :],
                                                       b_1[:, f:f + 1], sig[:, f % 2, :],
                                                       ALU.add, ALU.mult).then_inc(gated_ready, 1)
                for g in range(NG):
                    dve.wait_ge(x2_biased, NG * b + g + 1)
                    for i in range(2):
                        dve.wait_ge(down_ready, 2 * NG * b + 2 * g + i + 1)
                        pair = of_batch(x2, b, g * GT + 2 * i, 2)
                        nc.vector.tensor_tensor(
                            pair, banks[:, UP_BANKS + i, :].rearrange("p (c d) -> p c d", c=2), pair,
                            ALU.add).then_inc(y_ready, 1)

        @block.tensor
        def _(pe):
            def project(k):
                g = k % NG
                pe.wait_ge(ctxT_lo_ready, DC * k + DC)
                for i in range(2):
                    pe.wait_ge(x2_ready, 2 * k + i + 1)
                    for j in range(2):
                        t = 2 * i + j
                        for n, (left, right) in enumerate(EXACT):
                            for kc in range(DC):
                                last = nc.tensor.matmul(
                                    banks[:, 4 + 2 * g + i, j * D:(j + 1) * D],
                                    (ctxT_hi, ctxT_lo)[left][:, DC * g + kc, t * P:(t + 1) * P],
                                    (w_o_hi, w_o_lo)[right][:, kc, :],
                                    start=(n == 0 and kc == 0), stop=(n == len(EXACT) - 1 and kc == DC - 1))
                    last.then_inc(proj_ready, 1)

            back(pe, U - 1)
            def transpose_xn(k):
                b, g = divmod(k, NG)
                pe.wait_ge(xn_ready, k + 1)
                for c in range(DC):
                    for i in range(GT):
                        last = nc.tensor.transpose(banks[:, 4 * b + DC * g + c, i * P:(i + 1) * P],
                                                   xn[:, b, g * GT + i, c * P:(c + 1) * P], ident[:, :])
                last.then_inc(hT_ready, 1)

            pe.wait_ge(w_o_split, 1)
            project(0)
            pe.wait_ge(raw_saved, 1 + U)
            pe.wait_ge(ctx_stored, 1 + U)
            pe.wait_ge(ctxT_lo_ready, DC * NG)
            transpose_ctx(pe, 2)
            project(1)
            transpose_ctx(pe, 3)
            project(2)
            transpose_xn(0)
            project(3)
            pe.wait_ge(ctxT_lo_ready, DC * GROUPS)
            transpose_xn(1)
            pe.wait_ge(x2_ready, 4 + 2 * GROUPS)
            transpose_xn(2)
            transpose_xn(3)
            pe.wait_ge(w_1_split, 1)
            pe.wait_ge(w_2_split, 1)
            with pe.Fori(0, B) as b:
                for g in range(NG):
                    pe.wait_ge(hT_split, DC * NG * b + DC * NG)
                    for f in range(FC):
                        pe.wait_ge(gated_ready, FC * NG * b + FC * g + f + 1)
                        for n, (left, right) in enumerate(EXACT):
                            for kc in range(DC):
                                h = (hT_hi, hT_lo)[right][:, bass.ds(b, 1), DC * g + kc, :]
                                last = nc.tensor.matmul(
                                    banks[:, f % UP_BANKS, :], (w_1_hi, w_1_lo)[left][:, kc, f * P:(f + 1) * P],
                                    h.rearrange("p o n -> p (o n)"),
                                    start=(n == 0 and kc == 0), stop=(n == len(EXACT) - 1 and kc == DC - 1))
                        last.then_inc(up_ready, 1)
                pe.wait_ge(hT_split, DC * GROUPS)
                for g in range(NG):
                    pe.wait_ge(gated_split, STAGED + FC * NG * b + FC * g + FC)
                    for i in range(2):
                        pe.wait_ge(y_ready, 2 * NG * b + 2 * g + i + 1)
                        for j in range(2):
                            t = 2 * i + j
                            for n, (left, right) in enumerate(EXACT):
                                for f in range(FC):
                                    last = nc.tensor.matmul(
                                        banks[:, UP_BANKS + i, j * D:(j + 1) * D],
                                        (gated_hi[g], gated_lo[g])[left][:, f, t * P:(t + 1) * P],
                                        (w_2_hi, w_2_lo)[right][:, f, :],
                                        start=(n == 0 and f == 0),
                                        stop=(n == len(EXACT) - 1 and f == FC - 1))
                        last.then_inc(down_ready, 1)


_INS = {
    "x": "x", "itok": "itok_B_34_63", "bias": "fside_Bx16xSxS_0", "mask": "mask_Bx1xSxS_bk0",
    "W_ada": "L0_cond_W_ada", "b_ada": "L0_cond_b_ada", "Wq": "L0_cond_Wq", "bq": "L0_cond_bq",
    "Wk": "L0_cond_Wk", "bk": "L0_cond_bk", "Wv": "L0_cond_Wv", "bv": "L0_cond_bv", "Wo": "L0_cond_Wo",
    "bo": "L0_cond_bo", "W1": "L0_cond_W1", "b1": "L0_cond_b1", "W2": "L0_cond_W2", "b2": "L0_cond_b2",
    "g2": "L0_cond_g2", "beta2": "L0_cond_beta2",
}


def kernel(**inputs):
    import concourse.bacc as bacc
    from concourse.bass_utils import run_bass_kernel_spmd

    arrays = {short: np.ascontiguousarray(inputs[name]) for short, name in _INS.items()}
    arrays["bias"] = arrays["bias"].reshape(U, S, S)
    arrays["mask"] = arrays["mask"].reshape(B, S, S)
    half = D // 2
    arrays["freqs"] = np.exp(np.arange(half, dtype=np.float32) * np.float32(-math.log(10000.0) / (half - 1)))
    arrays["ident"] = np.eye(P, dtype=np.float32)

    nc = bacc.Bacc("TRN2", target_bir_lowering=False, num_devices=1)
    aps = {n: nc.dram_tensor(f"in_{n}", v.shape, mybir.dt.from_np(v.dtype), kind="ExternalInput").ap()
           for n, v in arrays.items()}
    out = nc.dram_tensor("out_x", (B, S, D), F32, kind="ExternalOutput").ap()
    layer_kernel(nc, aps, out)
    r = run_bass_kernel_spmd(nc, [{f"in_{n}": v for n, v in arrays.items()}], core_ids=[0])
    return r.results[0]["out_x"]
```
